# Optimizing a Trainium2 kernel written in Bass

```python
import numpy as np
import jax
import jax.numpy as jnp

def _softmax(x, axis=-1):
    return jax.nn.softmax(x, axis=axis)

def _gelu(x):
    return jax.nn.gelu(x, approximate=True)

def _silu(x):
    return jax.nn.silu(x)

def _sigmoid(x):
    return jax.nn.sigmoid(x)

def _layernorm(x, axis=-1, eps=1e-05):
    m = jnp.mean(x, axis=axis, keepdims=True)
    v = jnp.var(x, axis=axis, keepdims=True)
    return (x - m) / jnp.sqrt(v + eps)

def _scatter_add(tgt, idx, src, axis=0):
    return tgt.at[idx].add(src)

def _segment_sum(src, seg, n):
    return jax.ops.segment_sum(src, seg, n)
kernel_name = 'mk_gnn_preln_d2_gnn_r64_4d50fd'

def setup_inputs(seed: int=0):
    np.random.seed(seed)
    _w = jnp.asarray

    def _rec_inputs():
        import jax
        import jax.numpy as jnp
        _gk = jax.random.key(seed)
        x = -0.0003713 + 1 * jax.random.normal(jax.random.fold_in(_gk, 1), (100000, 128), jnp.float32)
        _s = jax.random.randint(jax.random.fold_in(_gk, 2), (25000,), 0, 100000, jnp.int32)
        _d = jax.random.randint(jax.random.fold_in(_gk, 3), (25000,), 0, 100000, jnp.int32)
        _loop = jnp.arange(100000, dtype=jnp.int32)
        src = jnp.concatenate([_s, _d, _loop])
        dst = jnp.concatenate([_d, _s, _loop])
        _o = jnp.argsort(dst, stable=True)
        src = src[_o]
        dst = dst[_o]
        edge_attr_16 = 0.00028786 + 0.999816 * jax.random.normal(jax.random.fold_in(_gk, 12), (3300000, 16), jnp.float32)
        return (x, src, dst, edge_attr_16)
    x, src, dst, edge_attr_16 = _rec_inputs()

    def _L0_gnn_setup():
        import jax, jax.numpy as jnp
        import numpy as np
        N_NODES = 100000
        N_EDGES = 9375
        D = 128

        def _sage_layer(x, src, dst, Wl, bl, Wr):
            msg = x[src]
            ssum = jax.ops.segment_sum(msg, dst, num_segments=N_NODES)
            deg = jax.ops.segment_sum(jnp.ones((msg.shape[0],), x.dtype), dst, num_segments=N_NODES)
            mean = ssum / jnp.clip(deg, 1.0)[:, None]
            return mean @ Wl + bl + x @ Wr
        key = jax.random.key(seed)
        ks = jax.random.split(key, 12)
        x = jax.random.normal(ks[0], (N_NODES, D), dtype=jnp.float32)
        edge_index = jax.random.randint(ks[1], (2, N_EDGES), 0, N_NODES, dtype=jnp.int64)
        edge_attr = jax.random.normal(ks[2], (N_EDGES, 16), dtype=jnp.float32)
        s = 1.0 / np.sqrt(D)
        params = {}
        for i, base in zip(range(3), (3, 6, 9)):
            params[f'Wl{i + 1}'] = jax.random.uniform(ks[base], (D, D), jnp.float32, -s, s)
            params[f'bl{i + 1}'] = jax.random.uniform(ks[base + 1], (D,), jnp.float32, -s, s)
            params[f'Wr{i + 1}'] = jax.random.uniform(ks[base + 2], (D, D), jnp.float32, -s, s)
        return {'x': x, 'edge_index': edge_index, 'edge_attr': edge_attr, **params}
    _L0_gnn_all = _L0_gnn_setup()
    _L0_gnn_in = {k: v for k, v in _L0_gnn_all.items() if k in ('Wl1', 'bl1', 'Wr1', 'Wl2', 'bl2', 'Wr2', 'Wl3', 'bl3', 'Wr3')}
    del _L0_gnn_all

    def _L1_gnn_setup():
        import jax, jax.numpy as jnp
        import numpy as np
        N_NODES = 100000
        N_RAND_EDGES = 25000
        D = 128

        def _graph_conv(x, W, b, src, dst, norm_src, norm_dst, n_nodes, act):
            h = x @ W
            m = h[src] * norm_src[:, None]
            agg = jax.ops.segment_sum(m, dst, num_segments=n_nodes)
            out = agg * norm_dst[:, None] + b
            return jax.nn.relu(out) if act else out
        key = jax.random.key(seed)
        k_feat, k_src, k_dst, k_w1, k_w2, k_w3 = jax.random.split(key, 6)
        feats = jax.random.normal(k_feat, (N_NODES, D), dtype=jnp.float32)
        src_r = jax.random.randint(k_src, (N_RAND_EDGES,), 0, N_NODES, dtype=jnp.int64)
        dst_r = jax.random.randint(k_dst, (N_RAND_EDGES,), 0, N_NODES, dtype=jnp.int64)
        loops = jnp.arange(N_NODES, dtype=jnp.int64)
        src = jnp.concatenate([src_r, loops])
        dst = jnp.concatenate([dst_r, loops])
        scale = 1.0 / np.sqrt(D)
        W1 = jax.random.normal(k_w1, (D, D), dtype=jnp.float32) * scale
        W2 = jax.random.normal(k_w2, (D, D), dtype=jnp.float32) * scale
        W3 = jax.random.normal(k_w3, (D, D), dtype=jnp.float32) * scale
        b1 = jnp.zeros((D,), dtype=jnp.float32)
        b2 = jnp.zeros((D,), dtype=jnp.float32)
        b3 = jnp.zeros((D,), dtype=jnp.float32)
        return {'feats': feats, 'W1': W1, 'b1': b1, 'W2': W2, 'b2': b2, 'W3': W3, 'b3': b3, 'src': src, 'dst': dst}
    _L1_gnn_all = _L1_gnn_setup()
    _L1_gnn_in = {k: v for k, v in _L1_gnn_all.items() if k in ('W1', 'b1', 'W2', 'b2', 'W3', 'b3')}
    del _L1_gnn_all
    return {'x': x, 'src': src, 'dst': dst, 'edge_attr_16': edge_attr_16, 'L0_gnn_Wl1': _L0_gnn_in['Wl1'], 'L0_gnn_bl1': _L0_gnn_in['bl1'], 'L0_gnn_Wr1': _L0_gnn_in['Wr1'], 'L0_gnn_Wl2': _L0_gnn_in['Wl2'], 'L0_gnn_bl2': _L0_gnn_in['bl2'], 'L0_gnn_Wr2': _L0_gnn_in['Wr2'], 'L0_gnn_Wl3': _L0_gnn_in['Wl3'], 'L0_gnn_bl3': _L0_gnn_in['bl3'], 'L0_gnn_Wr3': _L0_gnn_in['Wr3'], 'L1_gnn_W1': _L1_gnn_in['W1'], 'L1_gnn_b1': _L1_gnn_in['b1'], 'L1_gnn_W2': _L1_gnn_in['W2'], 'L1_gnn_b2': _L1_gnn_in['b2'], 'L1_gnn_W3': _L1_gnn_in['W3'], 'L1_gnn_b3': _L1_gnn_in['b3']}

def reference(x, src, dst, edge_attr_16, L0_gnn_Wl1, L0_gnn_bl1, L0_gnn_Wr1, L0_gnn_Wl2, L0_gnn_bl2, L0_gnn_Wr2, L0_gnn_Wl3, L0_gnn_bl3, L0_gnn_Wr3, L1_gnn_W1, L1_gnn_b1, L1_gnn_W2, L1_gnn_b2, L1_gnn_W3, L1_gnn_b3):
    import jax
    import jax.numpy as jnp

    def _L0_gnn_ref(x, edge_index, edge_attr, Wl1, bl1, Wr1, Wl2, bl2, Wr2, Wl3, bl3, Wr3):
        import jax, jax.numpy as jnp
        import numpy as np
        N_NODES = 100000
        N_EDGES = 9375
        D = 128

        def _sage_layer(x, src, dst, Wl, bl, Wr):
            msg = x[src]
            ssum = jax.ops.segment_sum(msg, dst, num_segments=N_NODES)
            deg = jax.ops.segment_sum(jnp.ones((msg.shape[0],), x.dtype), dst, num_segments=N_NODES)
            mean = ssum / jnp.clip(deg, 1.0)[:, None]
            return mean @ Wl + bl + x @ Wr
        src, dst = (edge_index[0], edge_index[1])
        h = _sage_layer(x, src, dst, Wl1, bl1, Wr1)
        h = jax.nn.relu(h)
        h = _sage_layer(h, src, dst, Wl2, bl2, Wr2)
        h = jax.nn.relu(h)
        h = _sage_layer(h, src, dst, Wl3, bl3, Wr3)
        return h

    def _L1_gnn_ref(feats, W1, b1, W2, b2, W3, b3, src, dst):
        import jax, jax.numpy as jnp
        import numpy as np
        N_NODES = 100000
        N_RAND_EDGES = 25000
        D = 128

        def _graph_conv(x, W, b, src, dst, norm_src, norm_dst, n_nodes, act):
            h = x @ W
            m = h[src] * norm_src[:, None]
            agg = jax.ops.segment_sum(m, dst, num_segments=n_nodes)
            out = agg * norm_dst[:, None] + b
            return jax.nn.relu(out) if act else out
        n = feats.shape[0]
        ones = jnp.ones(src.shape[0], dtype=feats.dtype)
        deg_out = jnp.clip(jax.ops.segment_sum(ones, src, num_segments=n), 1.0)
        deg_in = jnp.clip(jax.ops.segment_sum(ones, dst, num_segments=n), 1.0)
        norm_src = jax.lax.rsqrt(deg_out)[src]
        norm_dst = jax.lax.rsqrt(deg_in)
        h = _graph_conv(feats, W1, b1, src, dst, norm_src, norm_dst, n, act=True)
        h = _graph_conv(h, W2, b2, src, dst, norm_src, norm_dst, n, act=True)
        h = _graph_conv(h, W3, b3, src, dst, norm_src, norm_dst, n, act=False)
        return h
    edge_index = jnp.stack([src, dst])
    h = jnp.maximum(_layernorm(x, axis=-1), 0.0)
    x = x + _L0_gnn_ref(h, edge_index, edge_attr_16, L0_gnn_Wl1, L0_gnn_bl1, L0_gnn_Wr1, L0_gnn_Wl2, L0_gnn_bl2, L0_gnn_Wr2, L0_gnn_Wl3, L0_gnn_bl3, L0_gnn_Wr3)
    h = jnp.maximum(_layernorm(x, axis=-1), 0.0)
    x = x + _L1_gnn_ref(h, L1_gnn_W1, L1_gnn_b1, L1_gnn_W2, L1_gnn_b2, L1_gnn_W3, L1_gnn_b3, src, dst)
    return x

_drawn_inputs = setup_inputs


def setup_inputs(seed=0):
    import zlib

    import numpy as np

    out = dict(_drawn_inputs(seed))
    spreads = {'L1_gnn_b1': (0.0, 0.1), 'L1_gnn_b2': (0.0, 0.1), 'L1_gnn_b3': (0.0, 0.1)}
    factors = {'L0_gnn_bl1': 4.18}
    for name, (base, spread) in spreads.items():
        noise = np.random.default_rng([zlib.crc32(name.encode()), seed]).standard_normal(out[name].shape)
        drawn = base * np.exp(spread * noise) if base else spread * noise
        out[name] = jnp.asarray(drawn.astype(out[name].dtype))
    for name, factor in factors.items():
        out[name] = (out[name] * factor).astype(out[name].dtype)
    return out
```

```python
from contextlib import ExitStack

import numpy as np
import concourse.bass as bass
from concourse import mybir

F32 = mybir.dt.float32
F16 = mybir.dt.float16
BF16 = mybir.dt.bfloat16
I32 = mybir.dt.int32
ALU = mybir.AluOpType
ACT = mybir.ActivationFunctionType
AX = mybir.AxisListType

P = 128
N = 100000
D = 128
E = 150000
RPP = 4
BLOCK = P * RPP
BLOCKS = -(-N // BLOCK)
NPAD = BLOCKS * BLOCK
TAIL = (N - (BLOCKS - 1) * BLOCK) // RPP
UN = 4
TURNS = BLOCKS // UN
GROUPS = 3
GSTART = [0, 171, 342, BLOCK]
GW = [GSTART[j + 1] - GSTART[j] for j in range(GROUPS)]
TILES = BLOCKS * GROUPS
GB = -(-TILES // P)
ROW = 300
ROWS = E // ROW
CAP = P - 1
COLS = BLOCKS * RPP
HALF = COLS // 2
KEY0 = 8500000.0
NOKEY = -16000000.0
OOB = 200000
CHP, CHW = 125, E // 125
ET = -(-E // P)
EPS = 1e-5
HT = 12
HTURNS = TILES // HT
GT = 4
assert BLOCKS % UN == 0 and TILES % HT == 0 and ET % GT == 0 and E % ROW == 0

C_IOTA, C_ID, C_LO, C_W, C_GS, C_LOWER = 0, COLS, COLS + P, COLS + P + GB, COLS + P + 2 * GB, COLS + P + 2 * GB + 3
C_ALL = C_LOWER + P


def shape_constants():
    c = np.zeros((P, C_ALL), np.float32)
    c[:, C_IOTA:C_IOTA + COLS] = np.arange(COLS)
    c[:, C_ID:C_ID + P] = np.eye(P)
    g = np.arange(GB)[None, :] * P + np.arange(P)[:, None]
    c[:, C_LO:C_LO + GB] = BLOCK * (g // GROUPS) + np.array(GSTART)[g % GROUPS]
    c[:, C_W:C_W + GB] = np.where(g < TILES, np.array(GW)[g % GROUPS], 0)
    c[:, C_GS:C_GS + GROUPS] = GSTART[:GROUPS]
    c[:, C_LOWER:C_LOWER + P] = np.tril(np.ones((P, P)), -1)
    return c


NORM, SAGE1, SAGE2, SAGE3, GCN1, GCN2, GCN3 = range(7)
LAYERS = [SAGE1, SAGE2, SAGE3, GCN1, GCN2, GCN3]
SAGES = [SAGE1, SAGE2, SAGE3]
STAGES = {
    "x_loaded": (16, range(7)),
    "idx_staged": (1, LAYERS),
    "gathered": (16 * GROUPS, LAYERS),
    "onehot": (1, LAYERS),
    "summed": (1, LAYERS),
    "sum_out": (1, LAYERS),
    "xt_out": (1, LAYERS),
    "dense": (1, LAYERS),
    "prod_out": (1, SAGES),
    "combined": (1, LAYERS),
    "res_added": (1, [SAGE3]),
    "moments": (1, [NORM, SAGE3]),
    "stats": (1, [NORM, SAGE3]),
    "std": (1, [NORM, SAGE3]),
    "inverse": (1, [NORM, SAGE3]),
    "scaled": (1, [SAGE3]),
    "rstd": (1, [NORM, SAGE3]),
    "out_ready": (1, range(7)),
    "stored": (16, range(7)),
    "res_loaded": (16, [SAGE3, GCN3]),
    "res_stored": (16, [SAGE3]),
    "agg_loaded": (16, LAYERS),
}


def done(stage, phase, turn):
    unit, phases = STAGES[stage]
    return (turn + ((1 if stage == "gathered" else 2) + TURNS * list(phases).index(phase))) * unit


def before(stage, phase, turn):
    unit, phases = STAGES[stage]
    ahead = len([p for p in phases if p < phase])
    return (turn + ((0 if stage == "gathered" else 1) + TURNS * ahead)) * unit


def build(nc, x, src, dst, consts, sage_w, sage_b, gcn_w, gcn_b, out):
    h_a = nc.dram_tensor("h_a", [NPAD, D], F32, kind="Internal").ap()
    h_b = nc.dram_tensor("h_b", [NPAD, D], F32, kind="Internal").ap()
    residual = nc.dram_tensor("residual", [NPAD, D], F32, kind="Internal").ap()
    agg = nc.dram_tensor("agg", [NPAD, D], F32, kind="Internal").ap()
    H_IN = {SAGE1: h_a, SAGE2: h_b, SAGE3: h_a, GCN1: h_b, GCN2: h_a, GCN3: h_b}
    H_OUT = {NORM: h_a, SAGE1: h_b, SAGE2: h_a, SAGE3: h_b, GCN1: h_a, GCN2: h_b}

    def rows(array, block):
        v = array.rearrange("(s p i) d -> s p (i d)", p=P, i=RPP)
        return v[bass.ds(block, 1)].rearrange("s p f -> (s p) f")

    def tail_rows(array):
        return array[(BLOCKS - 1) * BLOCK:N, :].rearrange("(p i) d -> p (i d)", i=RPP)

    with ExitStack() as ctx:
        def sb(name, shape, dt=F32):
            return ctx.enter_context(nc.sbuf_tensor(name, shape, dt))

        def sem(name):
            return ctx.enter_context(nc.semaphore(name))

        bank = [ctx.enter_context(nc.psum_tensor(f"bank{k}", [P, 512], F32)) for k in range(8)]
        slot_sum, x_t, prod, prod_x = bank[0:2], bank[2:4], bank[4:6], bank[6:8]

        cst = sb("cst", [P, C_ALL])
        ident = cst[:, C_ID:C_ID + P]
        iota = cst[:, C_IOTA:C_IOTA + COLS]
        iota16 = sb("iota16", [P, COLS], F16)
        ones = sb("ones", [P, P])
        ones16 = sb("ones16", [96, P], BF16)
        w_l = [sb(f"w_l{k}", [P, D]) for k in range(3)]
        w_r = [sb(f"w_r{k}", [P, D]) for k in range(3)]
        w_g = [sb(f"w_g{k}", [P, D]) for k in range(3)]
        b_g = [sb(f"b_g{k}", [P, D]) for k in range(3)]
        b_row = sb("b_row", [96, 3, D])
        b_cut = sb("b_cut", [96, 3, D], BF16)
        b_parts = sb("b_parts", [96, 3, RPP * D], BF16)
        eps = sb("eps", [P, 1])

        slot_src = sb("slot_src", [P, GB * P], I32)
        slot_place = sb("slot_place", [P, GB * P])
        inv_deg = sb("inv_deg", [P, COLS])
        norm_dst = sb("norm_dst", [P, COLS])
        norm_src = sb("norm_src", [P, COLS])
        deg_in = sb("deg_in", [P, COLS])
        deg_out = sb("deg_out", [P, COLS])
        flag = sb("flag", [1, 1], I32)

        def four(name, shape, dt=F32):
            return [sb(f"{name}{k}", shape, dt) for k in range(UN)]

        x_rows = four("x_rows", [P, RPP * D])
        slot_rows = four("slot_rows", [P, GROUPS, D])
        onehot = four("onehot", [P, BLOCK])
        sum_t = four("sum_t", [P, BLOCK])
        xt_sb = four("xt_sb", [P, BLOCK])
        part = four("part", [P, RPP * D])
        res_rows = four("res_rows", [P, RPP * D])
        result = four("result", [P, RPP * D])
        idx = four("idx", [P, GROUPS], I32)
        bn6 = four("bn6", [P, RPP, 6])
        mv = four("mv", [P, RPP, 2])
        std = four("std", [P, RPP])
        scale = four("scale", [P, RPP])
        shift = four("shift", [P, RPP])

        s = {name: [sem(f"{name}{k}") for k in range(UN)] for name in STAGES}

        s_cst, s_w, s_edges, s_first = sem("s_cst"), sem("s_w"), sem("s_edges"), sem("s_first")
        s_clear, s_firstb, s_rows, s_win = sem("s_clear"), sem("s_firstb"), sem("s_rows"), sem("s_win")
        s_chk, s_chksum, s_flag, s_ready = sem("s_chk"), sem("s_chksum"), sem("s_flag"), sem("s_ready")
        s_top, s_slots = sem("s_top"), sem("s_slots")
        s_keys, s_keys_t = sem("s_keys"), sem("s_keys_t")
        s_oh = [sem(f"s_oh{k}") for k in range(4)]
        s_oh_used = [sem(f"s_oh_used{k}") for k in range(4)]
        s_h4, s_h4_out = sem("s_h4"), sem("s_h4_out")
        s_hist, s_sq, s_sqrt, s_tables = sem("s_hist"), sem("s_sq"), sem("s_sqrt"), sem("s_tables")
        s_dve, s_passed = sem("s_dve"), {e: sem(f"s_passed_{e}") for e in ("sp", "pool", "dve")}
        s_gload, s_zero, s_stage, s_eq = sem("s_gload"), sem("s_zero"), sem("s_stage"), sem("s_eq")
        s_spread, s_tot, s_new = sem("s_spread"), sem("s_tot"), sem("s_new")
        s_gath = [sem(f"s_gath{n}") for n in range(len(LAYERS))]
        s_scat = [sem(f"s_scat{n}") for n in range(len(LAYERS))]

        PREP_W = GB * ROW * 2
        win_dst = sb("win_dst", [P, GB, 2 * ROW + 1], I32)
        win_src = sb("win_src", [P, GB, 2 * ROW], I32)
        wa = sb("wa", [P, PREP_W])
        wb = sb("wb", [P, PREP_W])
        keys = sb("keys", [P, PREP_W])
        top = sb("top", [P, GB, P])
        small = sb("small", [P, 8 * GB])
        row_idx = sb("row_idx", [P, 2 * GB], I32)
        check3 = sb("check3", [P, 4])
        counts3 = sb("counts3", [1, 8])
        oh_p = [sb(f"oh_p{k}", [P, P], F16) for k in range(4)]
        oh_c = [sb(f"oh_c{k}", [P, COLS], F16) for k in range(4)]
        oh_q = [sb(f"oh_q{k}", [P, P], F16) for k in range(4)]
        oh_d = [part[k][:, 0:HALF].bitcast(F16) for k in range(4)]
        oh_r = sb("oh_r", [P, TILES, RPP], F16)
        zero16 = sb("zero16", [1, 512], F16)

        def w3(t):
            return t[:, :].rearrange("p (g w) -> p g w", g=GB)

        e_dst = wa[0:CHP, 0:CHW].bitcast(I32)
        e_next = wb[0:CHP, 0:CHW].bitcast(I32)
        e_src = keys[0:CHP, 0:CHW].bitcast(I32)
        e_tmp = wa[0:CHP, CHW:2 * CHW]
        e_tmp2 = wb[0:CHP, CHW:2 * CHW]
        first_row = keys[0:1, 2 * CHW:2 * CHW + ROWS].bitcast(I32)
        first_f = sb("first_f", [1, ROWS])
        g_src = wa[:, 0:ET].bitcast(I32)
        g_dst = wa[:, ET:2 * ET].bitcast(I32)
        g_dstf = wb[:, 0:ET]
        g_sp, g_sc = wb[:, ET:2 * ET], keys[:, 0:ET]
        g_dp, g_dc = keys[:, ET:2 * ET], win_src[:, :, :].rearrange("p g w -> p (g w)")[:, 0:ET].bitcast(F32)
        g_t1 = win_dst[:, :, :].rearrange("p g w -> p (g w)")[:, 0:ET]
        g_t2 = win_dst[:, :, :].rearrange("p g w -> p (g w)")[:, ET:2 * ET]
        kd = keys[:, 0:GB * P]
        kt = [wa[:, k * GB * P:(k + 1) * GB * P] for k in range(4)]
        ku = [wb[:, k * GB * P:(k + 1) * GB * P] for k in range(4)]
        src_p, src_c, dst_p = [keys[:, (k + 1) * GB * P:(k + 1) * GB * P + TILES] for k in range(3)]
        dst_c = ku[3][:, 0:TILES]
        top8 = sb("top8", [P, GB, 8])

        block = ctx.enter_context(nc.Block())

        def for_blocks(eng, stages, phase):
            most = max(a for a, _ in stages)
            for k in range(most):
                for a, stage in stages:
                    if k >= most - a:
                        n = k - (most - a)
                        stage(n // UN, n % UN, n, False)

            def turn(t, last):
                for k in range(UN):
                    for a, stage in stages:
                        up, slot = divmod(k + a, UN)
                        if last and t + up >= TURNS:
                            continue
                        stage(t + up, slot, t * UN + (k + a), last and t + up == TURNS - 1 and slot == UN - 1)

            peeled = 1 if most <= UN else 2
            with eng.Fori(0, TURNS - peeled) as t:
                turn(t, False)
            for t in range(TURNS - peeled, TURNS):
                turn(t, True)

        def wait_bank_free(eng, stage, phase, t, k):
            if k >= 2:
                eng.wait_ge(s[stage][k - 2], done(stage, phase, t))
            else:
                eng.wait_ge(s[stage][k + 2], before(stage, phase, t))

        def if_slots(eng, fast, general):
            eng.wait_ge(s_flag, 1)
            good = eng.value_load(flag[0:1, 0:1], min_val=0, max_val=1)
            with eng.If(good > 0):
                fast()
            with eng.Else():
                general()
            eng.end_ifs()
            eng.nop()

        def passed(eng, name):
            eng.sem_inc(s_passed[name], 1)

        def credit(eng, names):
            for name in names:
                for k in range(UN):
                    eng.sem_inc(s[name][k], STAGES[name][0])

        @block.sync
        def _(sp):
            credit(sp, ["x_loaded", "stored", "res_loaded", "res_stored", "agg_loaded"])
            sp.dma_start(cst[:, :], consts).then_inc(s_cst, 16)
            with nc.allow_non_contiguous_dma(reason="the first edge of each row of 300"):
                sp.dma_start(first_row, dst.rearrange("(a r w) -> a r w", a=1, w=ROW)[:, :, 0:1]
                             .rearrange("a r w -> a (r w)")).then_inc(s_first, 16)
            sp.wait_ge(s_clear, 1)
            sp.dma_start(e_dst, dst.rearrange("(p w) -> p w", p=CHP)).then_inc(s_edges, 16)
            sp.dma_start(e_src, src.rearrange("(p w) -> p w", p=CHP)).then_inc(s_edges, 16)
            sp.dma_start(e_next[0:CHP - 1, :], dst[1:1 + (CHP - 1) * CHW].rearrange("(p w) -> p w", p=CHP - 1)).then_inc(s_edges, 16)
            sp.dma_start(e_next[CHP - 1:CHP, 0:CHW - 1], dst[1 + (CHP - 1) * CHW:E].rearrange("(p w) -> p w", p=1)).then_inc(s_edges, 16)
            for k in range(3):
                sp.dma_start(w_l[k][:, :], sage_w[2 * k]).then_inc(s_w, 16)
                sp.dma_start(w_r[k][:, :], sage_w[2 * k + 1]).then_inc(s_w, 16)
                sp.dma_start(w_g[k][:, :], gcn_w[k]).then_inc(s_w, 16)
                sp.dma_start(b_g[k][:, :], gcn_b[k].partition_broadcast(P)).then_inc(s_w, 16)
                sp.dma_start(b_row[:, k, :], sage_b[k].partition_broadcast(96)).then_inc(s_w, 16)

            def phase(ph, general):
                if ph != NORM:
                    for k in range(UN):
                        sp.wait_ge(s["stored"][k], before("stored", ph, 0))
                if ph == GCN3:
                    for k in range(UN):
                        sp.wait_ge(s["res_stored"][k], done("res_stored", SAGE3, TURNS - 1))
                if ph != NORM and general:
                    sp.wait_ge(s_scat[LAYERS.index(ph)], 16 * ET)

                def load(t, k, b, last):
                    if ph == NORM:
                        sp.wait_ge(s["out_ready"][k], before("out_ready", ph, t))
                        if last:
                            sp.dma_start(x_rows[k][0:TAIL, :], tail_rows(x)).then_inc(s["x_loaded"][k], 16)
                        else:
                            sp.dma_start(x_rows[k][:, :], rows_x(b)).then_inc(s["x_loaded"][k], 16)
                        return
                    sp.wait_ge(s["summed"][k], before("summed", ph, t))
                    sp.dma_start(x_rows[k][:, :], rows(H_IN[ph], b)).then_inc(s["x_loaded"][k], 16)
                    if general:
                        sp.dma_start(onehot[k][:, :], rows(agg, b)).then_inc(s["agg_loaded"][k], 16)

                def load_residual(t, k, b, last):
                    if ph == SAGE3:
                        sp.wait_ge(s["res_stored"][k], before("res_stored", ph, t))
                        passed(sp, "sp")
                        sp.wait_ge(s["out_ready"][k], before("out_ready", ph, t))
                        passed(sp, "sp")
                        if last:
                            sp.dma_start(res_rows[k][0:TAIL, :], tail_rows(x)).then_inc(s["res_loaded"][k], 16)
                        else:
                            sp.dma_start(res_rows[k][:, :], rows_x(b)).then_inc(s["res_loaded"][k], 16)
                    if ph == GCN3:
                        sp.wait_ge(s["combined"][k], before("combined", ph, t))
                        sp.dma_start(res_rows[k][:, :], rows(residual, b)).then_inc(s["res_loaded"][k], 16)

                def store(t, k, b, last):
                    if ph == SAGE3:
                        sp.wait_ge(s["res_added"][k], done("res_added", ph, t))
                        sp.dma_start(rows(residual, b), res_rows[k][:, :]).then_inc(s["res_stored"][k], 16)
                    sp.wait_ge(s["out_ready"][k], done("out_ready", ph, t))
                    if ph != GCN3:
                        sp.dma_start(rows(H_OUT[ph], b), result[k][:, :]).then_inc(s["stored"][k], 16)
                    elif last:
                        sp.dma_start(tail_rows(out), result[k][0:TAIL, :]).then_inc(s["stored"][k], 16)
                    else:
                        sp.dma_start(rows_out(b), result[k][:, :]).then_inc(s["stored"][k], 16)

                if ph == NORM:
                    stages = [(3, load), (0, store)]
                elif ph in (SAGE3, GCN3):
                    stages = [(5, load), (3, load_residual), (0, store)]
                else:
                    stages = [(5, load), (0, store)]
                for_blocks(sp, stages, ph)

            def whole_blocks(array):
                return array[0:(BLOCKS - 1) * BLOCK, :]

            def rows_x(b):
                return rows(whole_blocks(x), b)

            def rows_out(b):
                return rows(whole_blocks(out), b)

            phase(NORM, False)

            def fast():
                for ph in LAYERS:
                    phase(ph, False)
                for k in range(UN):
                    sp.wait_ge(s["stored"][k], done("stored", GCN3, TURNS - 1))

            def general():
                sp.wait_ge(s_clear, 2)
                for a, g in ((src, g_src), (dst, g_dst)):
                    sp.dma_start(g[0:P - 1, :], a[0:(P - 1) * ET].rearrange("(p w) -> p w", p=P - 1)).then_inc(s_gload, 16)
                    sp.dma_start(g[P - 1:P, 0:E - (P - 1) * ET], a[(P - 1) * ET:E].rearrange("(p w) -> p w", p=1)).then_inc(s_gload, 16)
                for ph in LAYERS:
                    for k in range(UN):
                        sp.wait_ge(s["stored"][k], before("stored", ph, 0))
                    sp.wait_ge(s_clear, 3 + LAYERS.index(ph))
                    with sp.Fori(0, BLOCKS) as b:
                        sp.dma_start(rows(agg, b), onehot[0][:, :]).then_inc(s_zero, 16)
                        sp.wait_ge(s_zero, (b + (1 + BLOCKS * LAYERS.index(ph))) * 16)
                        passed(sp, "sp")
                    phase(ph, True)
                for k in range(UN):
                    sp.wait_ge(s["stored"][k], done("stored", GCN3, TURNS - 1))

            if_slots(sp, fast, general)

        @block.gpsimd
        def _(pool):
            pool.wait_ge(s_rows, 1)
            for g in range(GB):
                for half in range(2):
                    at = bass.IndirectOffsetOnAxis(ap=row_idx[:, 2 * g + half:2 * g + half + 1], axis=0)
                    for array, win in ((dst, win_dst), (src, win_src)):
                        pool.indirect_dma_start(win[:, g, half * ROW:(half + 1) * ROW], None,
                                                array.rearrange("(r w) -> r w", w=ROW), at,
                                                bounds_check=ROWS - 1, oob_is_err=False).then_inc(s_win, 16)

            def fast():
                for ph in LAYERS:
                    for k in range(UN):
                        pool.wait_ge(s["stored"][k], before("stored", ph, 0))

                    def gather(t, k, b, last):
                        pool.wait_ge(s["idx_staged"][k], done("idx_staged", ph, t))
                        passed(pool, "pool")
                        pool.wait_ge(s["summed"][k], before("summed", ph, t))
                        passed(pool, "pool")
                        for j in range(GROUPS):
                            pool.indirect_dma_start(slot_rows[k][:, j, :], None, H_IN[ph][:, :],
                                                    bass.IndirectOffsetOnAxis(ap=idx[k][:, j:j + 1], axis=0),
                                                    bounds_check=N - 1, oob_is_err=False).then_inc(s["gathered"][k], 16)

                    for_blocks(pool, [(0, gather)], ph)

            def general():
                for ph in LAYERS:
                    n = LAYERS.index(ph)
                    pool.wait_ge(s_zero, 16 * BLOCKS * (n + 1))
                    with pool.Fori(0, ET) as e:
                        pool.wait_ge(s_stage, e + (1 + n * ET))
                        passed(pool, "pool")
                        pool.indirect_dma_start(slot_rows[0][:, 0, :], None, H_IN[ph][:, :],
                                                bass.IndirectOffsetOnAxis(ap=idx[0][:, 0:1], axis=0),
                                                bounds_check=N - 1, oob_is_err=False).then_inc(s_gath[n], 16)
                        pool.indirect_dma_start(slot_rows[0][:, 1, :], None, agg[:, :],
                                                bass.IndirectOffsetOnAxis(ap=idx[0][:, 1:2], axis=0),
                                                bounds_check=N - 1, oob_is_err=False).then_inc(s_gath[n], 16)
                        pool.wait_ge(s_new, e + (1 + n * ET))
                        passed(pool, "pool")
                        pool.indirect_dma_start(agg[:, :], bass.IndirectOffsetOnAxis(ap=idx[1][:, 0:1], axis=0),
                                                slot_rows[1][:, 0, :], None,
                                                bounds_check=N - 1, oob_is_err=False).then_inc(s_scat[n], 16)

            if_slots(pool, fast, general)

        @block.scalar
        def _(act):
            credit(act, ["idx_staged", "xt_out", "prod_out", "std", "out_ready"])

            def phase(ph, general):
                def stage_idx(t, k, b, last):
                    if not (ph == SAGE1 and isinstance(t, int) and t == 0):
                        act.wait_ge(s["gathered"][k], before("gathered", ph, t))
                    act.copy(idx[k][:, :], slot_src[:, bass.ds(b * GROUPS, GROUPS)]).then_inc(s["idx_staged"][k], 1)

                def rows_out_t(t, k, b, last):
                    act.wait_ge(s["summed"][k], done("summed", ph, t))
                    act.wait_ge(s["dense"][k], before("dense", ph, t))
                    act.copy(xt_sb[k][:, :], x_t[k % 2][:, :]).then_inc(s["xt_out"][k], 1)

                def prod_out(t, k, b, last):
                    act.wait_ge(s["dense"][k], done("dense", ph, t))
                    if ph == SAGE3:
                        act.wait_ge(s["res_added"][k], before("res_added", ph, t))
                    for i in range(RPP):
                        at = slice(i * D, (i + 1) * D)
                        last_op = act.activation(part[k][:, at], prod[k % 2][:, at], ACT.Copy,
                                                 scale=inv_deg[:, bass.ds(b * RPP + i, 1)])
                    last_op.then_inc(s["prod_out"][k], 1)

                def deviation(t, k, b, last):
                    act.wait_ge(s["stats"][k], done("stats", ph, t))
                    act.wait_ge(s["rstd"][k], before("rstd", ph, t))
                    act.activation(std[k][:, :], mv[k][:, :, 1], ACT.Sqrt, bias=eps[:, 0:1]).then_inc(s["std"][k], 1)

                def finish(t, k, b, last):
                    act.wait_ge(s["stored"][k], before("stored", ph, t))
                    if ph in (NORM, SAGE3):
                        act.wait_ge(s["rstd"][k], done("rstd", ph, t))
                        rows_in = x_rows if ph == NORM else res_rows
                        for i in range(RPP):
                            at = slice(i * D, (i + 1) * D)
                            last_op = act.activation(result[k][:, at], rows_in[k][:, at], ACT.Relu,
                                                     bias=shift[k][:, i:i + 1], scale=scale[k][:, i:i + 1])
                        last_op.then_inc(s["out_ready"][k], 1)
                    elif ph in SAGES:
                        act.wait_ge(s["combined"][k], done("combined", ph, t))
                        act.activation(result[k][:, :], part[k][:, :], ACT.Relu).then_inc(s["out_ready"][k], 1)
                    else:
                        act.wait_ge(s["combined"][k], done("combined", ph, t))
                        for i in range(RPP):
                            at = slice(i * D, (i + 1) * D)
                            last_op = act.activation(result[k][:, at], part[k][:, at], ACT.Relu,
                                                     scale=norm_src[:, bass.ds(b * RPP + i, 1)])
                        last_op.then_inc(s["out_ready"][k], 1)

                if ph == NORM:
                    act.wait_ge(s_ready, 1)
                    for_blocks(act, [(1, deviation), (0, finish)], ph)
                    return
                if ph == SAGE3:
                    stages = [(7, stage_idx), (3, rows_out_t), (2, prod_out), (1, deviation), (0, finish)]
                elif ph in SAGES:
                    stages = [(6, stage_idx), (2, rows_out_t), (1, prod_out), (0, finish)]
                elif ph != GCN3:
                    stages = [(6, stage_idx), (2, rows_out_t), (0, finish)]
                else:
                    stages = [(6, stage_idx), (2, rows_out_t)]
                if general:
                    stages = stages[1:]
                for_blocks(act, stages, ph)

            phase(NORM, False)

            def roots():
                act.wait_ge(s_sq, 1)
                act.activation(norm_dst[:, :], deg_in[:, :], ACT.Sqrt).then_inc(s_sqrt, 1)
                act.activation(norm_src[:, :], deg_out[:, :], ACT.Sqrt).then_inc(s_sqrt, 1)
                act.wait_ge(s_tables, 1)

            def fast():
                roots()
                for ph in LAYERS:
                    phase(ph, False)

            def general():
                roots()
                for ph in LAYERS:
                    phase(ph, True)

            if_slots(act, fast, general)

        @block.vector
        def _(dve):
            credit(dve, ["onehot", "sum_out", "combined", "res_added", "moments", "stats", "inverse", "scaled", "rstd"])
            dve.sem_inc(s_h4_out, 1)
            count = [0]

            def start(ins):
                count[0] += 1
                ins.then_inc(s_dve, 1)

            def settle():
                dve.wait_ge(s_dve, count[0])

            def step(ins):
                start(ins)
                settle()

            def begin():
                start(dve.memset(eps[:, :], EPS))
                dve.memset(wb[:, 0:CHW].bitcast(I32), OOB).then_inc(s_clear, 1)
                start(dve.memset(ones[:, :], 1.0))
                start(dve.memset(ones16[:, :], 1.0))
                start(dve.memset(zero16[:, :], 0.0))
                start(dve.memset(check3[:, :], 0.0))
                start(dve.memset(win_dst[:, :, :], -1))
                start(dve.memset(win_src[:, :, :], 0))
                start(dve.memset(b_parts[:, :, :], 0.0))
                for k in range(UN):
                    start(dve.memset(slot_rows[k][:, :, :], 0.0))
                dve.wait_ge(s_cst, 16)
                start(dve.tensor_copy(iota16[:, :], iota))
                dve.wait_ge(s_first, 16)
                settle()
                dve.tensor_copy(first_f[:, :], first_row).then_inc(s_ready, 1)
                dve.wait_ge(s_firstb, 1)
                for g in range(GB):
                    step(dve.tensor_scalar(wb[:, 2 * CHW:2 * CHW + ROWS], bank[0][:, 0:ROWS],
                                           cst[:, C_LO + g:C_LO + g + 1], 0.0, ALU.is_lt, ALU.add,
                                           accum_out=small[:, g:g + 1]))
                step(dve.tensor_scalar(small[:, GB:2 * GB], small[:, 0:GB], 1.0, 0.0, ALU.subtract, ALU.max))
                row_of = row_idx[:, :].rearrange("p (g h) -> p g h", h=2)
                start(dve.tensor_copy(row_of[:, :, 0], small[:, GB:2 * GB]))
                dve.tensor_scalar(row_of[:, :, 1], small[:, GB:2 * GB], 1.0, None, ALU.add).then_inc(s_rows, 1)

            def check_edges():
                dve.wait_ge(s_edges, 64)
                step(dve.tensor_tensor(e_tmp, e_dst, e_next, ALU.is_gt))
                step(dve.tensor_reduce(check3[0:CHP, 0:1], e_tmp, AX.X, ALU.add))
                step(dve.tensor_tensor(e_tmp, e_dst, e_next, ALU.not_equal))
                step(dve.tensor_tensor(e_tmp2, e_dst, e_src, ALU.is_equal))
                step(dve.tensor_tensor_reduce(e_tmp, e_tmp, e_tmp2, 1.0, 0.0, ALU.mult, ALU.add, check3[0:CHP, 1:2]))

            def make_keys():
                dve.wait_ge(s_win, 16 * 4 * GB)
                lo = cst[:, C_LO:C_LO + GB].unsqueeze(2).to_broadcast([P, GB, 2 * ROW])
                width = cst[:, C_W:C_W + GB].unsqueeze(2).to_broadcast([P, GB, 2 * ROW])
                w_dst, w_next, w_src = win_dst[:, :, 0:2 * ROW], win_dst[:, :, 1:2 * ROW + 1], win_src[:, :, :]
                kept, loop, key = w3(wa), w3(wb), w3(keys)
                step(dve.tensor_tensor(kept, w_dst, w_next, ALU.not_equal))
                step(dve.tensor_tensor(loop, w_dst, w_src, ALU.is_equal))
                step(dve.tensor_tensor(loop, kept, loop, ALU.mult))
                step(dve.tensor_tensor(key, w_dst, lo, ALU.subtract))
                step(dve.tensor_tensor(kept, key, width, ALU.is_lt))
                step(dve.scalar_tensor_tensor(kept, key, 0.0, kept, ALU.is_ge, ALU.mult))
                step(dve.tensor_tensor(kept, kept, loop, ALU.is_gt))
                step(dve.tensor_reduce(small[:, 0:GB], kept, AX.X, ALU.add))
                step(dve.tensor_scalar(small[:, GB:2 * GB], small[:, 0:GB], float(CAP), None, ALU.is_gt))
                dve.tensor_reduce(check3[:, 2:3], small[:, GB:2 * GB], AX.X, ALU.add).then_inc(s_chk, 1)
                step(dve.tensor_scalar(key, key, float(N), KEY0, ALU.mult, ALU.subtract))
                step(dve.tensor_tensor(key, key, w_src, ALU.add))
                step(dve.tensor_tensor(key, key, kept, ALU.mult))
                step(dve.tensor_scalar(kept, kept, 1.0, -NOKEY, ALU.subtract, ALU.mult))
                step(dve.tensor_tensor(key, key, kept, ALU.add))
                dve.wait_ge(s_chksum, 1)
                step(dve.tensor_copy(counts3[:, 0:3], bank[1][0:1, 0:3]))
                step(dve.tensor_scalar(counts3[:, 4:5], counts3[:, 1:2], float(N), None, ALU.is_equal))
                step(dve.tensor_tensor(counts3[:, 3:4], counts3[:, 0:1], counts3[:, 2:3], ALU.add))
                step(dve.tensor_scalar(counts3[:, 5:6], counts3[:, 3:4], 0.0, None, ALU.is_equal))
                dve.tensor_tensor(flag[:, :], counts3[:, 4:5], counts3[:, 5:6], ALU.mult).then_inc(s_flag, 1)

            def cut_biases():
                dve.wait_ge(s_w, 16 * 15)
                for r in range(3):
                    at = slice(32 * r, 32 * r + 1)
                    four_times = b_parts[at, :, :].rearrange("r l (i d) -> r l i d", i=RPP)
                    for i in range(RPP):
                        start(dve.tensor_copy(four_times[:, :, i, :], b_row[at, :, :]))
                    if r < 2:
                        step(dve.tensor_copy(b_cut[:, :, :], b_row[:, :, :]))
                        step(dve.tensor_tensor(b_row[:, :, :], b_row[:, :, :], b_cut[:, :, :], ALU.subtract))

            def pick_slots():
                key = w3(keys)
                dve.sem_inc(s_top, 2 * GB + 1)
                with dve.Fori(0, P // 8) as r:
                    dve.wait_ge(s_top, (r + 1) * (2 * GB + 1))
                    passed(dve, "dve")
                    for g in range(GB):
                        dve.max(top8[:, g, :], key[:, g, :]).then_inc(s_top, 1)
                    dve.wait_ge(s_top, (r + 1) * (2 * GB + 1) + GB)
                    passed(dve, "dve")
                    for g in range(GB):
                        dve.match_replace(key[:, g, :], top8[:, g, :], key[:, g, :], NOKEY).then_inc(s_top, 1)
                    dve.tensor_copy(top[:, :, bass.ds(r * 8, 8)], top8[:, :, :]).then_inc(s_top, 1)
                dve.wait_ge(s_top, (P // 8 + 1) * (2 * GB + 1))
                dve.sem_inc(s_keys, 1)
                dve.wait_ge(s_keys_t, 1)
                half = 4 * P
                start(dve.tensor_copy(kd[:, 0:half], bank[2][:, :]))
                step(dve.tensor_copy(kd[:, half:GB * P], bank[3][:, 0:GB * P - half]))
                place_i, place, rest, low = kt[0].bitcast(I32), kt[1], kt[2], kt[3]
                high, fix, gone = ku[0], ku[1], ku[2]
                step(dve.tensor_scalar(place_i, kd, KEY0 - N / 2, 1.0 / N, ALU.add, ALU.mult))
                step(dve.tensor_copy(place, place_i))
                step(dve.tensor_scalar(rest, place, float(N), KEY0, ALU.mult, ALU.subtract))
                step(dve.tensor_tensor(rest, kd, rest, ALU.subtract))
                start(dve.tensor_scalar(low, rest, 0.0, None, ALU.is_lt))
                step(dve.tensor_scalar(high, rest, float(N), None, ALU.is_ge))
                step(dve.tensor_tensor(fix, high, low, ALU.subtract))
                start(dve.tensor_tensor(place, place, fix, ALU.add))
                step(dve.scalar_tensor_tensor(rest, fix, -float(N), rest, ALU.mult, ALU.add))
                step(dve.tensor_scalar(gone, place, 0.0, None, ALU.is_lt))
                start(dve.scalar_tensor_tensor(slot_place[:, :], gone, -2000.0, place, ALU.mult, ALU.add))
                step(dve.scalar_tensor_tensor(rest, gone, float(OOB), rest, ALU.mult, ALU.add))
                dve.tensor_copy(slot_src[:, :], rest).then_inc(s_slots, 1)
                dve.wait_ge(s_slots, 1)

            def table_places(number_p, number_c, number, t1, t2):
                start(dve.tensor_scalar(t1, number, 2, P - 1, ALU.logical_shift_right, ALU.bitwise_and))
                step(dve.tensor_scalar(t2, number, 9, 2, ALU.logical_shift_right, ALU.logical_shift_left))
                step(dve.tensor_copy(number_p, t1))
                step(dve.tensor_scalar(t1, number, RPP - 1, None, ALU.bitwise_and))
                step(dve.tensor_tensor(number_c, t2, t1, ALU.add))

            def count_slots():
                t1, t2 = kt[0].bitcast(I32)[:, 0:TILES], kt[1].bitcast(I32)[:, 0:TILES]
                table_places(src_p, src_c, slot_src[:, 0:TILES], t1, t2)
                by_group = slot_place[:, 0:TILES].rearrange("p (b j) -> p b j", j=GROUPS)
                start_of = cst[:, C_GS:C_GS + GROUPS].unsqueeze(1).to_broadcast([P, BLOCKS, GROUPS])
                step(dve.tensor_tensor(kt[2][:, 0:TILES].rearrange("p (b j) -> p b j", j=GROUPS), by_group, start_of, ALU.add))
                step(dve.tensor_copy(t1, kt[2][:, 0:TILES]))
                start(dve.tensor_scalar(t2, t1, 2, None, ALU.arith_shift_right))
                step(dve.tensor_scalar(t1, t1, RPP - 1, None, ALU.bitwise_and))
                start(dve.tensor_copy(dst_p, t2))
                step(dve.tensor_copy(dst_c, t1))
                step(dve.tensor_tensor(oh_r[:, :, :], dst_c.unsqueeze(2).to_broadcast([P, TILES, RPP]),
                                       iota[:, 0:RPP].unsqueeze(1).to_broadcast([P, TILES, RPP]), ALU.is_equal))
                with dve.Fori(0, HTURNS) as h:
                    for u in range(HT):
                        k, n = u % 4, u // 4
                        dve.wait_ge(s_oh_used[k], h * (HT // 4) + (n + 1))
                        dve.tensor_scalar(oh_q[k][:, :], iota16[:, 0:P], dst_p[:, bass.ds(h * HT + u, 1)], None, ALU.is_equal)
                        dve.tensor_scalar(oh_p[k][:, :], iota16[:, 0:P], src_p[:, bass.ds(h * HT + u, 1)], None, ALU.is_equal)
                        dve.tensor_scalar(oh_c[k][:, :], iota16[:, :], src_c[:, bass.ds(h * HT + u, 1)], None, ALU.is_equal)\
                           .then_inc(s_oh[k], 1)
                    dve.wait_ge(s_h4, h + 1)
                    dve.tensor_copy(deg_in[:, bass.ds(h * 4 * RPP, 4 * RPP)], bank[4][:, 0:4 * RPP]).then_inc(s_h4_out, 1)
                dve.wait_ge(s_h4_out, HTURNS + 1)
                dve.wait_ge(s_hist, 1)
                start(dve.tensor_scalar(deg_in[:, :], deg_in[:, :], 1.0, None, ALU.add))
                start(dve.tensor_scalar(deg_out[:, 0:HALF], bank[6][:, 0:HALF], 1.0, None, ALU.add))
                step(dve.tensor_scalar(deg_out[:, HALF:COLS], bank[7][:, 0:HALF], 1.0, None, ALU.add))

            def count_edges():
                dve.memset(wa[:, 0:2 * ET].bitcast(I32), OOB).then_inc(s_clear, 1)
                dve.wait_ge(s_gload, 64)
                table_places(g_sp, g_sc, g_src, g_t1, g_t2)
                table_places(g_dp, g_dc, g_dst, g_t1, g_t2)
                step(dve.tensor_copy(g_dstf, g_dst))
                with dve.Fori(0, ET // GT) as h:
                    for k in range(GT):
                        dve.wait_ge(s_oh_used[k], h + 1)
                        dve.tensor_scalar(oh_p[k][:, :], iota16[:, 0:P], g_sp[:, bass.ds(h * GT + k, 1)], None, ALU.is_equal)
                        dve.tensor_scalar(oh_c[k][:, :], iota16[:, :], g_sc[:, bass.ds(h * GT + k, 1)], None, ALU.is_equal)
                        dve.tensor_scalar(oh_q[k][:, :], iota16[:, 0:P], g_dp[:, bass.ds(h * GT + k, 1)], None, ALU.is_equal)
                        dve.tensor_scalar(oh_d[k], iota16[:, :], g_dc[:, bass.ds(h * GT + k, 1)], None, ALU.is_equal)\
                           .then_inc(s_oh[k], 1)
                dve.wait_ge(s_hist, 1)
                for c in range(2):
                    at = slice(c * HALF, (c + 1) * HALF)
                    start(dve.tensor_scalar(deg_in[:, at], bank[4 + c][:, 0:HALF], 1.0, None, ALU.max))
                    step(dve.tensor_scalar(deg_out[:, at], bank[6 + c][:, 0:HALF], 1.0, None, ALU.max))

            def norms():
                dve.sem_inc(s_sq, 1)
                step(dve.reciprocal(inv_deg[:, :], deg_in[:, :]))
                dve.wait_ge(s_sqrt, 2)
                dve.reciprocal(norm_dst[:, :], norm_dst[:, :]).then_inc(s_tables, 1)
                dve.reciprocal(norm_src[:, :], norm_src[:, :]).then_inc(s_tables, 1)
                dve.wait_ge(s_tables, 2)

            def add_messages(ph):
                n = LAYERS.index(ph)
                if n:
                    for k in range(UN):
                        dve.wait_ge(s["stored"][k], before("stored", ph, 0))
                dve.memset(onehot[0][:, :], 0.0).then_inc(s_clear, 1)
                per = 6
                base = count[0]
                with dve.Fori(0, ET) as e:
                    dve.tensor_copy(idx[0][:, 0:1], g_src[:, bass.ds(e, 1)]).then_inc(s_dve, 1)
                    dve.tensor_copy(idx[0][:, 1:2], g_dst[:, bass.ds(e, 1)]).then_inc(s_dve, 1)
                    dve.wait_ge(s_dve, e * per + (base + 2))
                    dve.tensor_scalar(sum_t[0][:, 0:P], ones[:, :], g_dstf[:, bass.ds(e, 1)], None, ALU.mult).then_inc(s_stage, 1)
                    dve.wait_ge(s_spread, e + (n * ET + 1))
                    dve.tensor_scalar(sum_t[1][:, 0:P], bank[4][:, 0:P], g_dstf[:, bass.ds(e, 1)], None, ALU.is_equal).then_inc(s_dve, 1)
                    dve.wait_ge(s_dve, e * per + (base + 3))
                    dve.tensor_tensor_reduce(sum_t[2][:, 0:P], sum_t[1][:, 0:P], cst[:, C_LOWER:C_LOWER + P], 1.0, 0.0,
                                             ALU.mult, ALU.add, small[:, 0:1]).then_inc(s_eq, 1)
                    dve.wait_ge(s_eq, e + (n * ET + 1))
                    dve.tensor_scalar(small[:, 1:2], small[:, 0:1], 0.0, float(OOB), ALU.is_gt, ALU.mult).then_inc(s_dve, 1)
                    dve.wait_ge(s_dve, e * per + (base + 4))
                    dve.tensor_tensor(small[:, 2:3], small[:, 1:2], g_dstf[:, bass.ds(e, 1)], ALU.add).then_inc(s_dve, 1)
                    dve.wait_ge(s_dve, e * per + (base + 5))
                    dve.tensor_copy(idx[1][:, 0:1], small[:, 2:3]).then_inc(s_dve, 1)
                    dve.wait_ge(s_dve, e * per + (base + 6))
                    dve.wait_ge(s_tot, e + (n * ET + 1))
                    dve.tensor_tensor(slot_rows[1][:, 0, :], bank[5][:, 0:D], slot_rows[0][:, 1, :], ALU.add).then_inc(s_new, 1)
                    dve.wait_ge(s_scat[n], (e + 1) * 16)
                    passed(dve, "dve")
                count[0] += per * ET

            def phase(ph, general):
                l = LAYERS.index(ph) % 3 if ph != NORM else 0

                def slots_by_nodes(k, b, j):
                    return dve.tensor_scalar(onehot[k][:, GSTART[j]:GSTART[j + 1]], iota[:, 0:GW[j]],
                                             slot_place[:, bass.ds(b * GROUPS + j, 1)], None, ALU.is_equal)

                def first_onehot(t, k, b, last):
                    dve.wait_ge(s["summed"][k], before("summed", ph, t))
                    slots_by_nodes(k, b, 0)

                def other_onehots(t, k, b, last):
                    slots_by_nodes(k, b, 1)
                    slots_by_nodes(k, b, 2).then_inc(s["onehot"][k], 1)

                def sums_out(t, k, b, last):
                    dve.wait_ge(s["summed"][k], done("summed", ph, t))
                    dve.wait_ge(s["dense"][k], before("dense", ph, t))
                    if general:
                        ins = dve.tensor_copy(sum_t[k][:, :], slot_sum[k % 2][:, :])
                    else:
                        dve.wait_ge(s["xt_out"][k], done("xt_out", ph, t))
                        ins = dve.tensor_tensor(sum_t[k][:, :].rearrange("d (i p) -> d i p", i=RPP),
                                                slot_sum[k % 2][:, :].rearrange("d (p i) -> d i p", i=RPP),
                                                xt_sb[k][:, :].rearrange("d (i p) -> d i p", i=RPP), ALU.add)
                    ins.then_inc(s["sum_out"][k], 1)

                def combine(t, k, b, last):
                    dve.wait_ge(s["dense"][k], done("dense", ph, t))
                    if ph in (SAGE1, SAGE2, GCN1, GCN2):
                        dve.wait_ge(s["out_ready"][k], before("out_ready", ph, t))
                    if ph == GCN3:
                        dve.wait_ge(s["res_loaded"][k], done("res_loaded", ph, t))
                    if ph in SAGES:
                        dve.wait_ge(s["prod_out"][k], done("prod_out", ph, t))
                        dve.tensor_tensor(part[k][:, :], part[k][:, :], prod_x[k % 2][:, :], ALU.add)\
                           .then_inc(s["combined"][k], 1)
                        return
                    for i in range(RPP):
                        at = slice(i * D, (i + 1) * D)
                        other = res_rows[k][:, at] if ph == GCN3 else b_g[l][:, :]
                        last_op = dve.scalar_tensor_tensor(part[k][:, at], prod[k % 2][:, at],
                                                           norm_dst[:, bass.ds(b * RPP + i, 1)], other, ALU.mult, ALU.add)
                    last_op.then_inc(s["combined"][k], 1)

                def add_residual(t, k, b, last):
                    dve.wait_ge(s["combined"][k], done("combined", ph, t))
                    dve.wait_ge(s["res_loaded"][k], done("res_loaded", ph, t))
                    dve.tensor_tensor(res_rows[k][:, :], res_rows[k][:, :], part[k][:, :], ALU.add).then_inc(s["res_added"][k], 1)

                def add_bias(t, k, b, last):
                    dve.wait_ge(s["combined"][k], done("combined", ph, t))
                    dve.wait_ge(s["stored"][k], before("stored", ph, t))
                    dve.tensor_tensor(result[k][:, :].rearrange("p (i d) -> p i d", i=RPP),
                                      part[k][:, :].rearrange("p (i d) -> p i d", i=RPP),
                                      b_g[l][:, :].unsqueeze(1).to_broadcast([P, RPP, D]), ALU.add).then_inc(s["out_ready"][k], 1)

                def statistics(t, k, b, last):
                    if ph == NORM:
                        dve.wait_ge(s["x_loaded"][k], done("x_loaded", ph, t))
                        rows_in = x_rows
                    else:
                        dve.wait_ge(s["res_added"][k], done("res_added", ph, t))
                        rows_in = res_rows
                    dve.wait_ge(s["std"][k], before("std", ph, t))
                    for i in range(RPP):
                        last_op = dve.bn_stats(bn6[k][:, i, :], rows_in[k][:, i * D:(i + 1) * D])
                    last_op.then_inc(s["moments"][k], 1)

                def aggregate(t, k, b, last):
                    dve.wait_ge(s["moments"][k], done("moments", ph, t))
                    passed(dve, "dve")
                    for i in range(RPP):
                        last_op = dve.bn_aggr(mv[k][:, i, :], bn6[k][:, i, :])
                    last_op.then_inc(s["stats"][k], 1)

                def invert(t, k, b, last):
                    dve.wait_ge(s["std"][k], done("std", ph, t))
                    dve.wait_ge(s["out_ready"][k], before("out_ready", ph, t))
                    dve.reciprocal(scale[k][:, :], std[k][:, :]).then_inc(s["inverse"][k], 1)

                def scale_out(t, k, b, last):
                    dve.wait_ge(s["inverse"][k], done("inverse", ph, t))
                    dve.tensor_tensor(scale[k][:, :], scale[k][:, :], norm_src[:, bass.ds(b * RPP, RPP)], ALU.mult)\
                       .then_inc(s["scaled"][k], 1)

                def find_shift(t, k, b, last):
                    scaled = "scaled" if ph == SAGE3 else "inverse"
                    dve.wait_ge(s[scaled][k], done(scaled, ph, t))
                    dve.scalar_tensor_tensor(shift[k][:, :], mv[k][:, :, 0], -1.0, scale[k][:, :], ALU.mult, ALU.mult)\
                       .then_inc(s["rstd"][k], 1)

                if ph == NORM:
                    stages = [(2, statistics), (0, invert), (2, aggregate), (0, find_shift)]
                elif ph == SAGE3:
                    stages = [(2, sums_out), (0, aggregate), (1, combine), (4, first_onehot), (0, invert), (1, add_residual),
                              (0, scale_out), (4, other_onehots), (0, find_shift), (1, statistics)]
                else:
                    stages = [(2, first_onehot), (2, other_onehots), (1, sums_out), (0, combine)]
                    if ph == GCN3:
                        stages.append((0, add_bias))
                for_blocks(dve, [x for x in stages if not (general and x[1] in (first_onehot, other_onehots))], ph)

            begin()
            check_edges()
            make_keys()
            cut_biases()
            phase(NORM, False)
            steps_before = count[0]

            def fast():
                pick_slots()
                count_slots()
                norms()
                for ph in LAYERS:
                    phase(ph, False)

            def general():
                count[0] = steps_before
                count_edges()
                norms()
                for ph in LAYERS:
                    add_messages(ph)
                    phase(ph, True)

            if_slots(dve, fast, general)

        @block.tensor
        def _(pe):
            credit(pe, ["summed", "dense"])
            for k in range(4):
                pe.sem_inc(s_oh_used[k], 1)
            pe.wait_ge(s_ready, 1)
            pe.matmul(bank[0][:, 0:ROWS], ones[0:1, :], first_f[:, :], start=True, stop=True).then_inc(s_firstb, 1)
            pe.wait_ge(s_chk, 1)
            pe.matmul(bank[1][0:1, 0:3], ones[:, 0:1], check3[:, 0:3], start=True, stop=True).then_inc(s_chksum, 1)

            def open_counts(banks, stop=False):
                for c in banks:
                    last_op = pe.matmul(bank[c][:, 0:HALF], zero16[0:1, 0:P], zero16[0:1, 0:HALF], start=not stop, stop=stop,
                                        skip_group_check=True)
                return last_op

            def count_slots():
                pe.wait_ge(s_keys, 1)
                for g in range(GB):
                    last_op = pe.transpose(bank[2 + g // 4][:, (g % 4) * P:(g % 4 + 1) * P], top[:, g, :], ident)
                last_op.then_inc(s_keys_t, 1)
                open_counts((6, 7))
                with pe.Fori(0, HTURNS) as h:
                    pe.wait_ge(s_h4_out, h + 1)
                    for u in range(HT):
                        k, n = u % 4, u // 4
                        pe.wait_ge(s_oh[k], h * (HT // 4) + (n + 1))
                        first, last = u % GROUPS == 0, u % GROUPS == GROUPS - 1
                        at = (u // GROUPS) * RPP
                        q = pe.matmul(bank[4][:, at:at + RPP], oh_q[k][:, :],
                                      oh_r[:, bass.ds(h * HT + u, 1), :].rearrange("p t r -> p (t r)"),
                                      start=first, stop=last, skip_group_check=True)
                        for c in range(2):
                            o = pe.matmul(bank[6 + c][:, 0:HALF], oh_p[k][:, :], oh_c[k][:, c * HALF:(c + 1) * HALF],
                                          start=False, stop=False, skip_group_check=True)
                        o.then_inc(s_oh_used[k], 1)
                    q.then_inc(s_h4, 1)
                open_counts((6, 7), True).then_inc(s_hist, 1)

            def count_edges():
                open_counts((4, 5, 6, 7))
                with pe.Fori(0, ET // GT) as h:
                    for k in range(GT):
                        pe.wait_ge(s_oh[k], h + 1)
                        for c in range(2):
                            at = slice(c * HALF, (c + 1) * HALF)
                            pe.matmul(bank[6 + c][:, 0:HALF], oh_p[k][:, :], oh_c[k][:, at], start=False, stop=False, skip_group_check=True)
                            o = pe.matmul(bank[4 + c][:, 0:HALF], oh_q[k][:, :], oh_d[k][:, at], start=False, stop=False, skip_group_check=True)
                        o.then_inc(s_oh_used[k], 1)
                open_counts((4, 5, 6, 7), True).then_inc(s_hist, 1)

            def add_messages(ph):
                n = LAYERS.index(ph)
                with pe.Fori(0, ET) as e:
                    pe.wait_ge(s_stage, e + (n * ET + 1))
                    pe.matmul(bank[4][:, 0:P], sum_t[0][:, 0:P], ident, start=True, stop=True).then_inc(s_spread, 1)
                    pe.wait_ge(s_eq, e + (n * ET + 1))
                    pe.wait_ge(s_gath[n], (e + 1) * 32)
                    pe.matmul(bank[5][:, 0:D], sum_t[1][:, 0:P], slot_rows[0][:, 0, :], start=True, stop=True).then_inc(s_tot, 1)

            def phase(ph, general):
                l = LAYERS.index(ph) % 3

                def front(t, k, b, last):
                    x_k, s_k = x_t[k % 2], slot_sum[k % 2]
                    pe.wait_ge(s["x_loaded"][k], done("x_loaded", ph, t))
                    wait_bank_free(pe, "sum_out", ph, t, k)
                    wait_bank_free(pe, "xt_out", ph, t, k)
                    for i in range(RPP):
                        at = slice(i * P, (i + 1) * P)
                        pe.transpose(x_k[:, at], x_rows[k][:, at], ident)
                    if general:
                        pe.wait_ge(s["agg_loaded"][k], done("agg_loaded", ph, t))
                        for i in range(RPP):
                            at = slice(i * P, (i + 1) * P)
                            last_op = pe.transpose(s_k[:, at], onehot[k][:, at], ident)
                    else:
                        pe.wait_ge(s["onehot"][k], done("onehot", ph, t))
                        pe.wait_ge(s["gathered"][k], done("gathered", ph, t))
                        for j in range(GROUPS):
                            at = slice(GSTART[j], GSTART[j + 1])
                            last_op = pe.matmul(s_k[:, at], slot_rows[k][:, j, :], onehot[k][:, at], start=True, stop=True)
                    last_op.then_inc(s["summed"][k], 1)

                def dense(t, k, b, last):
                    pe.wait_ge(s["sum_out"][k], done("sum_out", ph, t))
                    wait_bank_free(pe, "combined", ph, t, k)
                    w = w_l[l] if ph in SAGES else w_g[l]
                    for i in range(RPP):
                        at = slice(i * P, (i + 1) * P)
                        last_op = pe.matmul(prod[k % 2][:, at], sum_t[k][:, at], w[:, :], start=True, stop=True)
                    if ph in SAGES:
                        pe.wait_ge(s["xt_out"][k], done("xt_out", ph, t))
                        pe.matmul(prod_x[k % 2][:, :], ones16[:, :], b_parts[:, l, :], start=True, stop=False,
                                  skip_group_check=True)
                        for i in range(RPP):
                            at = slice(i * P, (i + 1) * P)
                            last_op = pe.matmul(prod_x[k % 2][:, at], xt_sb[k][:, at], w_r[l][:, :], start=False, stop=True,
                                                skip_group_check=True)
                    last_op.then_inc(s["dense"][k], 1)

                for_blocks(pe, [(1, front), (0, dense)], ph)

            def fast():
                count_slots()
                pe.wait_ge(s_tables, 2)
                for ph in LAYERS:
                    phase(ph, False)

            def general():
                count_edges()
                pe.wait_ge(s_tables, 2)
                for ph in LAYERS:
                    add_messages(ph)
                    phase(ph, True)

            if_slots(pe, fast, general)


_WEIGHTS = ["L0_gnn_Wl1", "L0_gnn_Wr1", "L0_gnn_Wl2", "L0_gnn_Wr2", "L0_gnn_Wl3", "L0_gnn_Wr3",
            "L1_gnn_W1", "L1_gnn_W2", "L1_gnn_W3"]
_BIASES = ["L0_gnn_bl1", "L0_gnn_bl2", "L0_gnn_bl3", "L1_gnn_b1", "L1_gnn_b2", "L1_gnn_b3"]


def make_program(nc):
    def given(name, shape, dt=F32):
        return nc.dram_tensor(name, shape, dt, kind="ExternalInput").ap()

    x, src, dst = given("x", [N, D]), given("src", [E], I32), given("dst", [E], I32)
    consts = given("consts", [P, C_ALL])
    w = [given(name, [D, D]) for name in _WEIGHTS]
    b = [given(name, [D]) for name in _BIASES]
    out = nc.dram_tensor("out", [N, D], F32, kind="ExternalOutput").ap()
    build(nc, x, src, dst, consts, w[0:6], b[0:3], w[6:9], b[3:6], out)


def kernel(**inputs):
    import concourse.bacc as bacc
    from concourse.bass_utils import run_bass_kernel_spmd

    nc = bacc.Bacc("TRN2", target_bir_lowering=False, num_devices=1)
    make_program(nc)
    arrays = {name: np.ascontiguousarray(inputs[name]) for name in ["x", "src", "dst"] + _WEIGHTS + _BIASES}
    arrays["consts"] = shape_constants()
    r = run_bass_kernel_spmd(nc, [arrays], core_ids=[0])
    return r.results[0]["out"]
```

```python
from contextlib import ExitStack

import numpy as np
import concourse.bass as bass
from concourse import mybir

F32 = mybir.dt.float32
F16 = mybir.dt.float16
BF16 = mybir.dt.bfloat16
I32 = mybir.dt.int32
ALU = mybir.AluOpType
ACT = mybir.ActivationFunctionType
AX = mybir.AxisListType

P = 128
N = 100000
D = 128
E = 150000
RPP = 4
BLOCK = P * RPP
BLOCKS = -(-N // BLOCK)
NPAD = BLOCKS * BLOCK
TAIL = (N - (BLOCKS - 1) * BLOCK) // RPP
UN = 4
TURNS = BLOCKS // UN
GROUPS = 3
GSTART = [0, 171, 342, BLOCK]
GW = [GSTART[j + 1] - GSTART[j] for j in range(GROUPS)]
TILES = BLOCKS * GROUPS
GB = -(-TILES // P)
ROW = 300
ROWS = E // ROW
CAP = P - 1
COLS = BLOCKS * RPP
HALF = COLS // 2
KEY0 = 8500000.0
NOKEY = -16000000.0
OOB = 200000
CHP, CHW = 125, E // 125
ET = -(-E // P)
EPS = 1e-5
GT = 4
assert BLOCKS % UN == 0 and UN * GROUPS % 4 == 0 and ET % GT == 0 and E % ROW == 0

C_IOTA, C_ID, C_LO, C_W, C_GS, C_LOWER = 0, COLS, COLS + P, COLS + P + GB, COLS + P + 2 * GB, COLS + P + 2 * GB + 3
C_ALL = C_LOWER + P


def shape_constants():
    c = np.zeros((P, C_ALL), np.float32)
    c[:, C_IOTA:C_IOTA + COLS] = np.arange(COLS)
    c[:, C_ID:C_ID + P] = np.eye(P)
    g = np.arange(GB)[None, :] * P + np.arange(P)[:, None]
    c[:, C_LO:C_LO + GB] = BLOCK * (g // GROUPS) + np.array(GSTART)[g % GROUPS]
    c[:, C_W:C_W + GB] = np.where(g < TILES, np.array(GW)[g % GROUPS], 0)
    c[:, C_GS:C_GS + GROUPS] = GSTART[:GROUPS]
    c[:, C_LOWER:C_LOWER + P] = np.tril(np.ones((P, P)), -1)
    return c


NORM, SAGE1, SAGE2, SAGE3, GCN1, GCN2, GCN3 = range(7)
LAYERS = [SAGE1, SAGE2, SAGE3, GCN1, GCN2, GCN3]
SAGES = [SAGE1, SAGE2, SAGE3]
STAGES = {
    "x_loaded": (16, range(7)),
    "idx_staged": (1, LAYERS),
    "gathered": (16 * GROUPS, LAYERS),
    "onehot": (1, LAYERS),
    "summed": (1, LAYERS),
    "sum_out": (1, LAYERS),
    "xt_out": (1, LAYERS),
    "dense": (1, LAYERS),
    "prod_out": (1, SAGES),
    "combined": (1, LAYERS),
    "res_added": (1, [SAGE3]),
    "moments": (1, [NORM, SAGE3]),
    "stats": (1, [NORM, SAGE3]),
    "std": (1, [NORM, SAGE3]),
    "inverse": (1, [NORM, SAGE3]),
    "scaled": (1, [SAGE3]),
    "rstd": (1, [NORM, SAGE3]),
    "out_ready": (1, range(7)),
    "stored": (16, range(7)),
    "res_loaded": (16, [SAGE3, GCN3]),
    "res_stored": (16, [SAGE3]),
    "agg_loaded": (16, LAYERS),
}


def done(stage, phase, turn):
    unit, phases = STAGES[stage]
    return (turn + ((1 if stage == "gathered" else 2) + TURNS * list(phases).index(phase))) * unit


def before(stage, phase, turn):
    unit, phases = STAGES[stage]
    ahead = len([p for p in phases if p < phase])
    return (turn + ((0 if stage == "gathered" else 1) + TURNS * ahead)) * unit


def build(nc, x, src, dst, consts, sage_w, sage_b, gcn_w, gcn_b, out):
    h_a = nc.dram_tensor("h_a", [NPAD, D], F32, kind="Internal").ap()
    h_b = nc.dram_tensor("h_b", [NPAD, D], F32, kind="Internal").ap()
    residual = nc.dram_tensor("residual", [NPAD, D], F32, kind="Internal").ap()
    agg = nc.dram_tensor("agg", [NPAD, D], F32, kind="Internal").ap()
    H_IN = {SAGE1: h_a, SAGE2: h_b, SAGE3: h_a, GCN1: h_b, GCN2: h_a, GCN3: h_b}
    H_OUT = {NORM: h_a, SAGE1: h_b, SAGE2: h_a, SAGE3: h_b, GCN1: h_a, GCN2: h_b}

    def rows(array, block):
        v = array.rearrange("(s p i) d -> s p (i d)", p=P, i=RPP)
        return v[bass.ds(block, 1)].rearrange("s p f -> (s p) f")

    def tail_rows(array):
        return array[(BLOCKS - 1) * BLOCK:N, :].rearrange("(p i) d -> p (i d)", i=RPP)

    with ExitStack() as ctx:
        def sb(name, shape, dt=F32):
            return ctx.enter_context(nc.sbuf_tensor(name, shape, dt))

        def sem(name):
            return ctx.enter_context(nc.semaphore(name))

        bank = [ctx.enter_context(nc.psum_tensor(f"bank{k}", [P, 512], F32)) for k in range(8)]
        slot_sum, x_t, prod, prod_x = bank[0:2], bank[2:4], bank[4:6], bank[6:8]

        cst = sb("cst", [P, C_ALL])
        ident = cst[:, C_ID:C_ID + P]
        iota = cst[:, C_IOTA:C_IOTA + COLS]
        iota16 = sb("iota16", [P, COLS], F16)
        ones = sb("ones", [P, P])
        ones16 = sb("ones16", [96, P], BF16)
        w_l = [sb(f"w_l{k}", [P, D]) for k in range(3)]
        w_r = [sb(f"w_r{k}", [P, D]) for k in range(3)]
        w_g = [sb(f"w_g{k}", [P, D]) for k in range(3)]
        b_g = [sb(f"b_g{k}", [P, D]) for k in range(3)]
        b_s = [sb(f"b_s{k}", [P, D]) for k in range(2)]
        b_row = sb("b_row", [96, D])
        b_cut = sb("b_cut", [96, D], BF16)
        b_parts = sb("b_parts", [96, RPP * D], BF16)
        eps = sb("eps", [P, 1])

        slot_src = sb("slot_src", [P, GB * P], I32)
        slot_place = sb("slot_place", [P, GB * P])
        inv_deg = sb("inv_deg", [P, COLS])
        norm_dst = sb("norm_dst", [P, COLS])
        norm_src = sb("norm_src", [P, COLS])
        deg_in = sb("deg_in", [P, COLS])
        deg_out = sb("deg_out", [P, COLS])
        flag = sb("flag", [1, 1], I32)

        def four(name, shape, dt=F32):
            return [sb(f"{name}{k}", shape, dt) for k in range(UN)]

        x_rows = four("x_rows", [P, RPP * D])
        slot_rows = four("slot_rows", [P, GROUPS, D])
        onehot = four("onehot", [P, BLOCK])
        sum_t = four("sum_t", [P, BLOCK])
        xt_sb = four("xt_sb", [P, BLOCK])
        part = four("part", [P, RPP * D])
        res_rows = four("res_rows", [P, RPP * D])
        result = four("result", [P, RPP * D])
        idx = four("idx", [P, GROUPS], I32)
        bn6 = four("bn6", [P, RPP, 6])
        mv = four("mv", [P, RPP, 2])
        std = four("std", [P, RPP])
        scale = four("scale", [P, RPP])
        shift = four("shift", [P, RPP])

        s = {name: [sem(f"{name}{k}") for k in range(UN)] for name in STAGES}

        s_cst, s_w, s_edges, s_first = sem("s_cst"), sem("s_w"), sem("s_edges"), sem("s_first")
        s_clear, s_firstb, s_rows, s_win = sem("s_clear"), sem("s_firstb"), sem("s_rows"), sem("s_win")
        s_chk, s_chksum, s_flag, s_ready = sem("s_chk"), sem("s_chksum"), sem("s_flag"), sem("s_ready")
        s_top, s_slots = sem("s_top"), sem("s_slots")
        s_keys, s_keys_t = sem("s_keys"), sem("s_keys_t")
        s_oh = [sem(f"s_oh{k}") for k in range(4)]
        s_pq = [sem(f"s_pq{k}") for k in range(UN)]
        s_oh_used = [sem(f"s_oh_used{k}") for k in range(4)]
        s_degree, s_degree_out = sem("s_degree"), sem("s_degree_out")
        s_hist, s_sqrt, s_tables = sem("s_hist"), sem("s_sqrt"), sem("s_tables")
        s_dve, s_passed = sem("s_dve"), {e: sem(f"s_passed_{e}") for e in ("sp", "pool", "dve")}
        s_gload, s_zero, s_stage, s_eq = sem("s_gload"), sem("s_zero"), sem("s_stage"), sem("s_eq")
        s_spread, s_tot, s_new = sem("s_spread"), sem("s_tot"), sem("s_new")
        s_gath = [sem(f"s_gath{n}") for n in range(len(LAYERS))]
        s_scat = [sem(f"s_scat{n}") for n in range(len(LAYERS))]

        PREP_W = GB * ROW * 2
        win_dst = sb("win_dst", [P, GB, 2 * ROW + 1], I32)
        win_src = sb("win_src", [P, GB, 2 * ROW], I32)
        wa = sb("wa", [P, PREP_W])
        wb = sb("wb", [P, PREP_W])
        keys = sb("keys", [P, PREP_W])
        top = sb("top", [P, GB, P])
        small = sb("small", [P, 8 * GB])
        row_idx = sb("row_idx", [P, 2 * GB], I32)
        check3 = sb("check3", [P, 4])
        counts3 = sb("counts3", [1, 8])
        oh_pq = [sb(f"oh_pq{k}", [P, 2, GROUPS, P], F16) for k in range(UN)]
        oh_q, oh_p = [[t[:, h, 0, :] for t in oh_pq] for h in range(2)]
        oh_c = [sb(f"oh_c{k}", [P, COLS], F16) for k in range(4)]
        oh_d = [part[k][:, 0:HALF].bitcast(F16) for k in range(4)]
        oh_r = sb("oh_r", [P, TILES, RPP], F16)
        zero16 = sb("zero16", [1, 512], F16)

        def w3(t):
            return t[:, :].rearrange("p (g w) -> p g w", g=GB)

        e_dst = wa[0:CHP, 0:CHW].bitcast(I32)
        e_next = wb[0:CHP, 0:CHW].bitcast(I32)
        e_src = keys[0:CHP, 0:CHW].bitcast(I32)
        e_tmp = wa[0:CHP, CHW:2 * CHW]
        e_tmp2 = wb[0:CHP, CHW:2 * CHW]
        first_row = keys[0:1, 2 * CHW:2 * CHW + ROWS].bitcast(I32)
        first_f = sb("first_f", [1, ROWS])
        g_src = wa[:, 0:ET].bitcast(I32)
        g_dst = wa[:, ET:2 * ET].bitcast(I32)
        g_dstf = wb[:, 0:ET]
        g_sp, g_sc = wb[:, ET:2 * ET], keys[:, 0:ET]
        g_dp, g_dc = keys[:, ET:2 * ET], win_src[:, :, :].rearrange("p g w -> p (g w)")[:, 0:ET].bitcast(F32)
        g_t1 = win_dst[:, :, :].rearrange("p g w -> p (g w)")[:, 0:ET]
        g_t2 = win_dst[:, :, :].rearrange("p g w -> p (g w)")[:, ET:2 * ET]
        kd = keys[:, 0:GB * P]
        kt = [wa[:, k * GB * P:(k + 1) * GB * P] for k in range(4)]
        ku = [wb[:, k * GB * P:(k + 1) * GB * P] for k in range(4)]
        src_c = keys[:, GB * P:GB * P + TILES]
        place_pq = sb("place_pq", [P, 2, TILES], F16)
        dst_p, src_p = place_pq[:, 0, :], place_pq[:, 1, :]
        dst_c = ku[3][:, 0:TILES]
        top8 = sb("top8", [P, GB, 8])

        block = ctx.enter_context(nc.Block())

        def for_blocks(eng, stages, phase):
            most = max(a for a, _ in stages)
            for k in range(most):
                for a, stage in stages:
                    if k >= most - a:
                        n = k - (most - a)
                        stage(n // UN, n % UN, n, False)

            def turn(t, last):
                for k in range(UN):
                    for a, stage in stages:
                        up, slot = divmod(k + a, UN)
                        if last and t + up >= TURNS:
                            continue
                        stage(t + up, slot, t * UN + (k + a), last and t + up == TURNS - 1 and slot == UN - 1)

            peeled = 1 if most <= UN else 2
            with eng.Fori(0, TURNS - peeled) as t:
                turn(t, False)
            for t in range(TURNS - peeled, TURNS):
                turn(t, True)

        def wait_bank_free(eng, stage, phase, t, k):
            if k >= 2:
                eng.wait_ge(s[stage][k - 2], done(stage, phase, t))
            else:
                eng.wait_ge(s[stage][k + 2], before(stage, phase, t))

        def if_slots(eng, fast, general):
            eng.wait_ge(s_flag, 1)
            good = eng.value_load(flag[0:1, 0:1], min_val=0, max_val=1)
            with eng.If(good > 0):
                fast()
            with eng.Else():
                general()
            eng.end_ifs()
            eng.nop()

        def passed(eng, name):
            eng.sem_inc(s_passed[name], 1)

        def credit(eng, names):
            for name in names:
                for k in range(UN):
                    eng.sem_inc(s[name][k], STAGES[name][0])

        @block.sync
        def _(sp):
            credit(sp, ["x_loaded", "stored", "res_loaded", "res_stored", "agg_loaded"])
            sp.dma_start(cst[:, :], consts).then_inc(s_cst, 16)
            with nc.allow_non_contiguous_dma(reason="the first edge of each row of 300"):
                sp.dma_start(first_row, dst.rearrange("(a r w) -> a r w", a=1, w=ROW)[:, :, 0:1]
                             .rearrange("a r w -> a (r w)")).then_inc(s_first, 16)
            sp.wait_ge(s_clear, 1)
            sp.dma_start(e_dst, dst.rearrange("(p w) -> p w", p=CHP)).then_inc(s_edges, 16)
            sp.dma_start(e_src, src.rearrange("(p w) -> p w", p=CHP)).then_inc(s_edges, 16)
            sp.dma_start(e_next[0:CHP - 1, :], dst[1:1 + (CHP - 1) * CHW].rearrange("(p w) -> p w", p=CHP - 1)).then_inc(s_edges, 16)
            sp.dma_start(e_next[CHP - 1:CHP, 0:CHW - 1], dst[1 + (CHP - 1) * CHW:E].rearrange("(p w) -> p w", p=1)).then_inc(s_edges, 16)
            for k in range(3):
                sp.dma_start(w_l[k][:, :], sage_w[2 * k]).then_inc(s_w, 16)
                sp.dma_start(w_r[k][:, :], sage_w[2 * k + 1]).then_inc(s_w, 16)
                sp.dma_start(w_g[k][:, :], gcn_w[k]).then_inc(s_w, 16)
                sp.dma_start(b_g[k][:, :], gcn_b[k].partition_broadcast(P)).then_inc(s_w, 16)
                sp.dma_start(b_s[k][:, :] if k < 2 else b_row[:, :],
                             sage_b[k].partition_broadcast(P if k < 2 else 96)).then_inc(s_w, 16)

            def phase(ph, general):
                if ph != NORM:
                    for k in range(UN):
                        sp.wait_ge(s["stored"][k], before("stored", ph, 0))
                if ph == GCN3:
                    for k in range(UN):
                        sp.wait_ge(s["res_stored"][k], done("res_stored", SAGE3, TURNS - 1))
                if ph != NORM and general:
                    sp.wait_ge(s_scat[LAYERS.index(ph)], 16 * ET)

                def load(t, k, b, last):
                    if ph == NORM:
                        sp.wait_ge(s["out_ready"][k], before("out_ready", ph, t))
                        if last:
                            sp.dma_start(x_rows[k][0:TAIL, :], tail_rows(x)).then_inc(s["x_loaded"][k], 16)
                        else:
                            sp.dma_start(x_rows[k][:, :], rows_x(b)).then_inc(s["x_loaded"][k], 16)
                        return
                    sp.wait_ge(s["summed"][k], before("summed", ph, t))
                    sp.dma_start(x_rows[k][:, :], rows(H_IN[ph], b)).then_inc(s["x_loaded"][k], 16)
                    if general:
                        sp.dma_start(onehot[k][:, :], rows(agg, b)).then_inc(s["agg_loaded"][k], 16)

                def load_residual(t, k, b, last):
                    if ph == SAGE3:
                        sp.wait_ge(s["res_stored"][k], before("res_stored", ph, t))
                        passed(sp, "sp")
                        sp.wait_ge(s["out_ready"][k], before("out_ready", ph, t))
                        passed(sp, "sp")
                        if last:
                            sp.dma_start(res_rows[k][0:TAIL, :], tail_rows(x)).then_inc(s["res_loaded"][k], 16)
                        else:
                            sp.dma_start(res_rows[k][:, :], rows_x(b)).then_inc(s["res_loaded"][k], 16)
                    if ph == GCN3:
                        sp.wait_ge(s["combined"][k], before("combined", ph, t))
                        sp.dma_start(res_rows[k][:, :], rows(residual, b)).then_inc(s["res_loaded"][k], 16)

                def store(t, k, b, last):
                    if ph == SAGE3:
                        sp.wait_ge(s["res_added"][k], done("res_added", ph, t))
                        sp.dma_start(rows(residual, b), res_rows[k][:, :]).then_inc(s["res_stored"][k], 16)
                    sp.wait_ge(s["out_ready"][k], done("out_ready", ph, t))
                    if ph != GCN3:
                        sp.dma_start(rows(H_OUT[ph], b), result[k][:, :]).then_inc(s["stored"][k], 16)
                    elif last:
                        sp.dma_start(tail_rows(out), result[k][0:TAIL, :]).then_inc(s["stored"][k], 16)
                    else:
                        sp.dma_start(rows_out(b), result[k][:, :]).then_inc(s["stored"][k], 16)

                if ph == NORM:
                    stages = [(3, load), (0, store)]
                elif ph in (SAGE3, GCN3):
                    stages = [(5, load), (3, load_residual), (0, store)]
                else:
                    stages = [(5, load), (0, store)]
                for_blocks(sp, stages, ph)

            def whole_blocks(array):
                return array[0:(BLOCKS - 1) * BLOCK, :]

            def rows_x(b):
                return rows(whole_blocks(x), b)

            def rows_out(b):
                return rows(whole_blocks(out), b)

            def fast():
                for ph in [NORM] + LAYERS:
                    phase(ph, False)
                for k in range(UN):
                    sp.wait_ge(s["stored"][k], done("stored", GCN3, TURNS - 1))

            def general():
                phase(NORM, True)
                sp.wait_ge(s_clear, 2)
                for a, g in ((src, g_src), (dst, g_dst)):
                    sp.dma_start(g[0:P - 1, :], a[0:(P - 1) * ET].rearrange("(p w) -> p w", p=P - 1)).then_inc(s_gload, 16)
                    sp.dma_start(g[P - 1:P, 0:E - (P - 1) * ET], a[(P - 1) * ET:E].rearrange("(p w) -> p w", p=1)).then_inc(s_gload, 16)
                for ph in LAYERS:
                    for k in range(UN):
                        sp.wait_ge(s["stored"][k], before("stored", ph, 0))
                    sp.wait_ge(s_clear, 3 + LAYERS.index(ph))
                    with sp.Fori(0, BLOCKS) as b:
                        sp.dma_start(rows(agg, b), onehot[0][:, :]).then_inc(s_zero, 16)
                        sp.wait_ge(s_zero, (b + (1 + BLOCKS * LAYERS.index(ph))) * 16)
                        passed(sp, "sp")
                    phase(ph, True)
                for k in range(UN):
                    sp.wait_ge(s["stored"][k], done("stored", GCN3, TURNS - 1))

            if_slots(sp, fast, general)

        @block.gpsimd
        def _(pool):
            pool.wait_ge(s_rows, 1)
            for g in range(GB):
                for half in range(2):
                    at = bass.IndirectOffsetOnAxis(ap=row_idx[:, 2 * g + half:2 * g + half + 1], axis=0)
                    for array, win in ((dst, win_dst), (src, win_src)):
                        pool.indirect_dma_start(win[:, g, half * ROW:(half + 1) * ROW], None,
                                                array.rearrange("(r w) -> r w", w=ROW), at,
                                                bounds_check=ROWS - 1, oob_is_err=False).then_inc(s_win, 16)

            def fast():
                for ph in LAYERS:
                    for k in range(UN):
                        pool.wait_ge(s["stored"][k], before("stored", ph, 0))

                    def gather(t, k, b, last):
                        pool.wait_ge(s["idx_staged"][k], done("idx_staged", ph, t))
                        passed(pool, "pool")
                        pool.wait_ge(s["summed"][k], before("summed", ph, t))
                        passed(pool, "pool")
                        for j in range(GROUPS):
                            pool.indirect_dma_start(slot_rows[k][:, j, :], None, H_IN[ph][:, :],
                                                    bass.IndirectOffsetOnAxis(ap=idx[k][:, j:j + 1], axis=0),
                                                    bounds_check=N - 1, oob_is_err=False).then_inc(s["gathered"][k], 16)

                    for_blocks(pool, [(0, gather)], ph)

            def general():
                for ph in LAYERS:
                    n = LAYERS.index(ph)
                    pool.wait_ge(s_zero, 16 * BLOCKS * (n + 1))
                    with pool.Fori(0, ET) as e:
                        pool.wait_ge(s_stage, e + (1 + n * ET))
                        passed(pool, "pool")
                        pool.indirect_dma_start(slot_rows[0][:, 0, :], None, H_IN[ph][:, :],
                                                bass.IndirectOffsetOnAxis(ap=idx[0][:, 0:1], axis=0),
                                                bounds_check=N - 1, oob_is_err=False).then_inc(s_gath[n], 16)
                        pool.indirect_dma_start(slot_rows[0][:, 1, :], None, agg[:, :],
                                                bass.IndirectOffsetOnAxis(ap=idx[0][:, 1:2], axis=0),
                                                bounds_check=N - 1, oob_is_err=False).then_inc(s_gath[n], 16)
                        pool.wait_ge(s_new, e + (1 + n * ET))
                        passed(pool, "pool")
                        pool.indirect_dma_start(agg[:, :], bass.IndirectOffsetOnAxis(ap=idx[1][:, 0:1], axis=0),
                                                slot_rows[1][:, 0, :], None,
                                                bounds_check=N - 1, oob_is_err=False).then_inc(s_scat[n], 16)

            if_slots(pool, fast, general)

        @block.scalar
        def _(act):
            credit(act, ["idx_staged", "xt_out", "prod_out", "std", "out_ready"])

            def phase(ph, general):
                def stage_idx(t, k, b, last):
                    if not (ph == SAGE1 and isinstance(t, int) and t == 0):
                        act.wait_ge(s["gathered"][k], before("gathered", ph, t))
                    act.copy(idx[k][:, :], slot_src[:, bass.ds(b * GROUPS, GROUPS)]).then_inc(s["idx_staged"][k], 1)

                def rows_out_t(t, k, b, last):
                    act.wait_ge(s["summed"][k], done("summed", ph, t))
                    act.wait_ge(s["dense"][k], before("dense", ph, t))
                    act.copy(xt_sb[k][:, :], x_t[k % 2][:, :]).then_inc(s["xt_out"][k], 1)

                def prod_out(t, k, b, last):
                    act.wait_ge(s["dense"][k], done("dense", ph, t))
                    act.wait_ge(s["res_added"][k], before("res_added", ph, t))
                    for i in range(RPP):
                        at = slice(i * D, (i + 1) * D)
                        last_op = act.activation(part[k][:, at], prod[k % 2][:, at], ACT.Copy,
                                                 scale=inv_deg[:, bass.ds(b * RPP + i, 1)])
                    last_op.then_inc(s["prod_out"][k], 1)

                def deviation(t, k, b, last):
                    act.wait_ge(s["stats"][k], done("stats", ph, t))
                    act.wait_ge(s["rstd"][k], before("rstd", ph, t))
                    act.activation(std[k][:, :], mv[k][:, :, 1], ACT.Sqrt, bias=eps[:, 0:1]).then_inc(s["std"][k], 1)

                def finish(t, k, b, last):
                    act.wait_ge(s["stored"][k], before("stored", ph, t))
                    if ph in (NORM, SAGE3):
                        act.wait_ge(s["rstd"][k], done("rstd", ph, t))
                        rows_in = x_rows if ph == NORM else res_rows
                        for i in range(RPP):
                            at = slice(i * D, (i + 1) * D)
                            last_op = act.activation(result[k][:, at], rows_in[k][:, at], ACT.Relu,
                                                     bias=shift[k][:, i:i + 1], scale=scale[k][:, i:i + 1])
                        last_op.then_inc(s["out_ready"][k], 1)
                    elif ph in SAGES:
                        act.wait_ge(s["combined"][k], done("combined", ph, t))
                        act.activation(result[k][:, :], part[k][:, :], ACT.Relu).then_inc(s["out_ready"][k], 1)
                    else:
                        act.wait_ge(s["combined"][k], done("combined", ph, t))
                        for i in range(RPP):
                            at = slice(i * D, (i + 1) * D)
                            last_op = act.activation(result[k][:, at], part[k][:, at], ACT.Relu,
                                                     scale=norm_src[:, bass.ds(b * RPP + i, 1)])
                        last_op.then_inc(s["out_ready"][k], 1)

                def in_degrees_out(t, k, b, last):
                    act.wait_ge(s_degree, t * UN + (k + 1))
                    act.copy(deg_in[:, bass.ds(b * RPP, RPP)], bank[2 + k][:, 0:RPP]).then_inc(s_degree_out, 1)

                if ph == NORM:
                    act.wait_ge(s_ready, 1)
                    stages = [(0, finish), (1, deviation)]
                    for_blocks(act, stages if general else stages + [(0, in_degrees_out)], ph)
                    return
                if ph == SAGE3:
                    stages = [(7, stage_idx), (3, rows_out_t), (2, prod_out), (1, deviation), (0, finish)]
                elif ph != GCN3:
                    stages = [(6, stage_idx), (2, rows_out_t), (0, finish)]
                else:
                    stages = [(6, stage_idx), (2, rows_out_t)]
                if general:
                    stages = stages[1:]
                for_blocks(act, stages, ph)

            def roots():
                act.wait_ge(s_tables, 1)
                act.activation(norm_dst[:, :], deg_in[:, :], ACT.Sqrt).then_inc(s_sqrt, 1)
                act.activation(norm_src[:, :], deg_out[:, :], ACT.Sqrt).then_inc(s_sqrt, 1)

            def layers(general):
                phase(NORM, general)
                roots()
                for ph in LAYERS:
                    if ph == SAGE3:
                        act.wait_ge(s_tables, 3)
                    phase(ph, general)

            def fast():
                layers(False)

            def general():
                layers(True)

            if_slots(act, fast, general)

        @block.vector
        def _(dve):
            credit(dve, ["onehot", "sum_out", "combined", "res_added", "moments", "stats", "inverse", "scaled", "rstd"])
            dve.sem_inc(s_degree_out, UN)
            count = [0]

            def start(ins):
                count[0] += 1
                ins.then_inc(s_dve, 1)

            def settle():
                dve.wait_ge(s_dve, count[0])

            def step(ins):
                start(ins)
                settle()

            def begin():
                start(dve.memset(eps[:, :], EPS))
                dve.memset(wb[:, 0:CHW].bitcast(I32), OOB).then_inc(s_clear, 1)
                start(dve.memset(ones[:, :], 1.0))
                start(dve.memset(ones16[:, :], 1.0))
                start(dve.memset(zero16[:, :], 0.0))
                start(dve.memset(check3[:, :], 0.0))
                start(dve.memset(win_dst[:, :, :], -1))
                start(dve.memset(win_src[:, :, :], 0))
                start(dve.memset(b_parts[:, :], 0.0))
                for k in range(UN):
                    start(dve.memset(slot_rows[k][:, :, :], 0.0))
                dve.wait_ge(s_cst, 16)
                start(dve.tensor_copy(iota16[:, :], iota))
                dve.wait_ge(s_first, 16)
                settle()
                dve.tensor_copy(first_f[:, :], first_row).then_inc(s_ready, 1)
                dve.wait_ge(s_firstb, 1)
                for g in range(GB):
                    step(dve.tensor_scalar(wb[:, 2 * CHW:2 * CHW + ROWS], bank[0][:, 0:ROWS],
                                           cst[:, C_LO + g:C_LO + g + 1], 0.0, ALU.is_lt, ALU.add,
                                           accum_out=small[:, g:g + 1]))
                step(dve.tensor_scalar(small[:, GB:2 * GB], small[:, 0:GB], 1.0, 0.0, ALU.subtract, ALU.max))
                row_of = row_idx[:, :].rearrange("p (g h) -> p g h", h=2)
                start(dve.tensor_copy(row_of[:, :, 0], small[:, GB:2 * GB]))
                dve.tensor_scalar(row_of[:, :, 1], small[:, GB:2 * GB], 1.0, None, ALU.add).then_inc(s_rows, 1)

            def check_edges():
                dve.wait_ge(s_edges, 64)
                step(dve.tensor_tensor(e_tmp, e_dst, e_next, ALU.is_gt))
                step(dve.tensor_reduce(check3[0:CHP, 0:1], e_tmp, AX.X, ALU.add))
                step(dve.tensor_tensor(e_tmp, e_dst, e_next, ALU.not_equal))
                step(dve.tensor_tensor(e_tmp2, e_dst, e_src, ALU.is_equal))
                step(dve.tensor_tensor_reduce(e_tmp, e_tmp, e_tmp2, 1.0, 0.0, ALU.mult, ALU.add, check3[0:CHP, 1:2]))

            def make_keys():
                dve.wait_ge(s_win, 16 * 4 * GB)
                lo = cst[:, C_LO:C_LO + GB].unsqueeze(2).to_broadcast([P, GB, 2 * ROW])
                width = cst[:, C_W:C_W + GB].unsqueeze(2).to_broadcast([P, GB, 2 * ROW])
                w_dst, w_next, w_src = win_dst[:, :, 0:2 * ROW], win_dst[:, :, 1:2 * ROW + 1], win_src[:, :, :]
                kept, loop, key = w3(wa), w3(wb), w3(keys)
                step(dve.tensor_tensor(kept, w_dst, w_next, ALU.not_equal))
                step(dve.tensor_tensor(loop, w_dst, w_src, ALU.is_equal))
                step(dve.tensor_tensor(loop, kept, loop, ALU.mult))
                step(dve.tensor_tensor(key, w_dst, lo, ALU.subtract))
                step(dve.tensor_tensor(kept, key, width, ALU.is_lt))
                step(dve.scalar_tensor_tensor(kept, key, 0.0, kept, ALU.is_ge, ALU.mult))
                step(dve.tensor_tensor(kept, kept, loop, ALU.is_gt))
                step(dve.tensor_reduce(small[:, 0:GB], kept, AX.X, ALU.add))
                step(dve.tensor_scalar(small[:, GB:2 * GB], small[:, 0:GB], float(CAP), None, ALU.is_gt))
                dve.tensor_reduce(check3[:, 2:3], small[:, GB:2 * GB], AX.X, ALU.add).then_inc(s_chk, 1)
                step(dve.tensor_scalar(key, key, float(N), KEY0, ALU.mult, ALU.subtract))
                step(dve.tensor_tensor(key, key, w_src, ALU.add))
                step(dve.tensor_tensor(key, key, kept, ALU.mult))
                step(dve.tensor_scalar(kept, kept, 1.0, -NOKEY, ALU.subtract, ALU.mult))
                step(dve.tensor_tensor(key, key, kept, ALU.add))
                dve.wait_ge(s_chksum, 1)
                step(dve.tensor_copy(counts3[:, 0:3], bank[1][0:1, 0:3]))
                step(dve.tensor_scalar(counts3[:, 4:5], counts3[:, 1:2], float(N), None, ALU.is_equal))
                step(dve.tensor_tensor(counts3[:, 3:4], counts3[:, 0:1], counts3[:, 2:3], ALU.add))
                step(dve.tensor_scalar(counts3[:, 5:6], counts3[:, 3:4], 0.0, None, ALU.is_equal))
                dve.tensor_tensor(flag[:, :], counts3[:, 4:5], counts3[:, 5:6], ALU.mult).then_inc(s_flag, 1)

            def cut_bias():
                dve.wait_ge(s_w, 16 * 15)
                for r in range(3):
                    at = slice(32 * r, 32 * r + 1)
                    for i in range(RPP):
                        start(dve.tensor_copy(b_parts[at, i * D:(i + 1) * D], b_row[at, :]))
                    if r < 2:
                        step(dve.tensor_copy(b_cut[:, :], b_row[:, :]))
                        step(dve.tensor_tensor(b_row[:, :], b_row[:, :], b_cut[:, :], ALU.subtract))

            def pick_slots():
                key = w3(keys)
                dve.sem_inc(s_top, 2 * GB + 1)
                with dve.Fori(0, P // 8) as r:
                    dve.wait_ge(s_top, (r + 1) * (2 * GB + 1))
                    passed(dve, "dve")
                    for g in range(GB):
                        dve.max(top8[:, g, :], key[:, g, :]).then_inc(s_top, 1)
                    dve.wait_ge(s_top, (r + 1) * (2 * GB + 1) + GB)
                    passed(dve, "dve")
                    for g in range(GB):
                        dve.match_replace(key[:, g, :], top8[:, g, :], key[:, g, :], NOKEY).then_inc(s_top, 1)
                    dve.tensor_copy(top[:, :, bass.ds(r * 8, 8)], top8[:, :, :]).then_inc(s_top, 1)
                dve.wait_ge(s_top, (P // 8 + 1) * (2 * GB + 1))
                dve.sem_inc(s_keys, 1)
                dve.wait_ge(s_keys_t, 1)
                half = 4 * P
                start(dve.tensor_copy(kd[:, 0:half], bank[2][:, :]))
                step(dve.tensor_copy(kd[:, half:GB * P], bank[3][:, 0:GB * P - half]))
                place_i, place, rest, low = kt[0].bitcast(I32), kt[1], kt[2], kt[3]
                high, fix, gone = ku[0], ku[1], ku[2]
                step(dve.tensor_scalar(place_i, kd, KEY0 - N / 2, 1.0 / N, ALU.add, ALU.mult))
                step(dve.tensor_copy(place, place_i))
                step(dve.tensor_scalar(rest, place, float(N), KEY0, ALU.mult, ALU.subtract))
                step(dve.tensor_tensor(rest, kd, rest, ALU.subtract))
                start(dve.tensor_scalar(low, rest, 0.0, None, ALU.is_lt))
                step(dve.tensor_scalar(high, rest, float(N), None, ALU.is_ge))
                step(dve.tensor_tensor(fix, high, low, ALU.subtract))
                start(dve.tensor_tensor(place, place, fix, ALU.add))
                step(dve.scalar_tensor_tensor(rest, fix, -float(N), rest, ALU.mult, ALU.add))
                step(dve.tensor_scalar(gone, place, 0.0, None, ALU.is_lt))
                start(dve.scalar_tensor_tensor(slot_place[:, :], gone, -2000.0, place, ALU.mult, ALU.add))
                step(dve.scalar_tensor_tensor(rest, gone, float(OOB), rest, ALU.mult, ALU.add))
                dve.tensor_copy(slot_src[:, :], rest).then_inc(s_slots, 1)
                dve.wait_ge(s_slots, 1)

            def table_places(number_p, number_c, number, t1, t2):
                start(dve.tensor_scalar(t1, number, 2, P - 1, ALU.logical_shift_right, ALU.bitwise_and))
                step(dve.tensor_scalar(t2, number, 9, 2, ALU.logical_shift_right, ALU.logical_shift_left))
                step(dve.tensor_copy(number_p, t1))
                step(dve.tensor_scalar(t1, number, RPP - 1, None, ALU.bitwise_and))
                step(dve.tensor_tensor(number_c, t2, t1, ALU.add))

            def place_slots():
                t1, t2 = kt[0].bitcast(I32)[:, 0:TILES], kt[1].bitcast(I32)[:, 0:TILES]
                table_places(src_p, src_c, slot_src[:, 0:TILES], t1, t2)
                by_group = slot_place[:, 0:TILES].rearrange("p (b j) -> p b j", j=GROUPS)
                start_of = cst[:, C_GS:C_GS + GROUPS].unsqueeze(1).to_broadcast([P, BLOCKS, GROUPS])
                step(dve.tensor_tensor(kt[2][:, 0:TILES].rearrange("p (b j) -> p b j", j=GROUPS), by_group, start_of, ALU.add))
                step(dve.tensor_copy(t1, kt[2][:, 0:TILES]))
                start(dve.tensor_scalar(t2, t1, 2, None, ALU.arith_shift_right))
                step(dve.tensor_scalar(t1, t1, RPP - 1, None, ALU.bitwise_and))
                start(dve.tensor_copy(dst_p, t2))
                step(dve.tensor_copy(dst_c, t1))
                step(dve.tensor_tensor(oh_r[:, :, :], dst_c.unsqueeze(2).to_broadcast([P, TILES, RPP]),
                                       iota[:, 0:RPP].unsqueeze(1).to_broadcast([P, TILES, RPP]), ALU.is_equal))

            def count_tile(j):
                def stage(t, k, b, last):
                    u = GROUPS * k + j
                    o = u % 4
                    if j == 0:
                        after = u + GROUPS - 1
                        dve.wait_ge(s_oh_used[after % 4], t * GROUPS + (after // 4 + 1))
                        dve.tensor_tensor(oh_pq[k][:, :, :, :], place_pq[:, :, bass.ds(b * GROUPS, GROUPS)].unsqueeze(3)
                                          .to_broadcast([P, 2, GROUPS, P]), iota16[:, 0:P].unsqueeze(1).unsqueeze(1)
                                          .to_broadcast([P, 2, GROUPS, P]), ALU.is_equal).then_inc(s_pq[k], 1)
                    dve.wait_ge(s_oh_used[o], t * GROUPS + (u // 4 + GROUPS))
                    dve.tensor_scalar(oh_c[o][:, :], iota16[:, :], src_c[:, bass.ds(b * GROUPS + j, 1)], None, ALU.is_equal)\
                       .then_inc(s_oh[o], 1)
                return stage

            def finish_counts():
                dve.wait_ge(s_degree_out, BLOCKS + UN)
                dve.wait_ge(s_hist, 1)
                start(dve.tensor_scalar(deg_in[:, :], deg_in[:, :], 1.0, None, ALU.add))
                start(dve.tensor_scalar(deg_out[:, 0:HALF], bank[6][:, 0:HALF], 1.0, None, ALU.add))
                step(dve.tensor_scalar(deg_out[:, HALF:COLS], bank[7][:, 0:HALF], 1.0, None, ALU.add))

            def count_edges():
                dve.memset(wa[:, 0:2 * ET].bitcast(I32), OOB).then_inc(s_clear, 1)
                dve.wait_ge(s_gload, 64)
                table_places(g_sp, g_sc, g_src, g_t1, g_t2)
                table_places(g_dp, g_dc, g_dst, g_t1, g_t2)
                step(dve.tensor_copy(g_dstf, g_dst))
                with dve.Fori(0, ET // GT) as h:
                    for k in range(GT):
                        dve.wait_ge(s_oh_used[k], h + GROUPS)
                        dve.tensor_scalar(oh_p[k][:, :], iota16[:, 0:P], g_sp[:, bass.ds(h * GT + k, 1)], None, ALU.is_equal)
                        dve.tensor_scalar(oh_c[k][:, :], iota16[:, :], g_sc[:, bass.ds(h * GT + k, 1)], None, ALU.is_equal)
                        dve.tensor_scalar(oh_q[k][:, :], iota16[:, 0:P], g_dp[:, bass.ds(h * GT + k, 1)], None, ALU.is_equal)
                        dve.tensor_scalar(oh_d[k], iota16[:, :], g_dc[:, bass.ds(h * GT + k, 1)], None, ALU.is_equal)\
                           .then_inc(s_oh[k], 1)
                dve.wait_ge(s_hist, 1)
                for c in range(2):
                    at = slice(c * HALF, (c + 1) * HALF)
                    start(dve.tensor_scalar(deg_in[:, at], bank[4 + c][:, 0:HALF], 1.0, None, ALU.max))
                    step(dve.tensor_scalar(deg_out[:, at], bank[6 + c][:, 0:HALF], 1.0, None, ALU.max))

            def invert_degrees():
                dve.reciprocal(inv_deg[:, :], deg_in[:, :]).then_inc(s_tables, 1)
                dve.wait_ge(s_tables, 1)

            def norms():
                dve.wait_ge(s_sqrt, 2)
                factor = keys[:, 0:COLS]
                for y, deg in ((norm_dst, deg_in), (norm_src, deg_out)):
                    step(dve.reciprocal(y[:, :], y[:, :]))
                    step(dve.tensor_tensor(factor, y[:, :], y[:, :], ALU.mult))
                    step(dve.tensor_tensor(factor, factor, deg[:, :], ALU.mult))
                    step(dve.tensor_scalar(factor, factor, -0.5, 1.5, ALU.mult, ALU.add))
                    dve.tensor_tensor(y[:, :], y[:, :], factor, ALU.mult).then_inc(s_tables, 1)
                    dve.wait_ge(s_tables, 2 if y is norm_dst else 3)

            def add_messages(ph):
                n = LAYERS.index(ph)
                if n:
                    for k in range(UN):
                        dve.wait_ge(s["stored"][k], before("stored", ph, 0))
                dve.memset(onehot[0][:, :], 0.0).then_inc(s_clear, 1)
                per = 6
                base = count[0]
                with dve.Fori(0, ET) as e:
                    dve.tensor_copy(idx[0][:, 0:1], g_src[:, bass.ds(e, 1)]).then_inc(s_dve, 1)
                    dve.tensor_copy(idx[0][:, 1:2], g_dst[:, bass.ds(e, 1)]).then_inc(s_dve, 1)
                    dve.wait_ge(s_dve, e * per + (base + 2))
                    dve.tensor_scalar(sum_t[0][:, 0:P], ones[:, :], g_dstf[:, bass.ds(e, 1)], None, ALU.mult).then_inc(s_stage, 1)
                    dve.wait_ge(s_spread, e + (n * ET + 1))
                    dve.tensor_scalar(sum_t[1][:, 0:P], bank[4][:, 0:P], g_dstf[:, bass.ds(e, 1)], None, ALU.is_equal).then_inc(s_dve, 1)
                    dve.wait_ge(s_dve, e * per + (base + 3))
                    dve.tensor_tensor_reduce(sum_t[2][:, 0:P], sum_t[1][:, 0:P], cst[:, C_LOWER:C_LOWER + P], 1.0, 0.0,
                                             ALU.mult, ALU.add, small[:, 0:1]).then_inc(s_eq, 1)
                    dve.wait_ge(s_eq, e + (n * ET + 1))
                    dve.tensor_scalar(small[:, 1:2], small[:, 0:1], 0.0, float(OOB), ALU.is_gt, ALU.mult).then_inc(s_dve, 1)
                    dve.wait_ge(s_dve, e * per + (base + 4))
                    dve.tensor_tensor(small[:, 2:3], small[:, 1:2], g_dstf[:, bass.ds(e, 1)], ALU.add).then_inc(s_dve, 1)
                    dve.wait_ge(s_dve, e * per + (base + 5))
                    dve.tensor_copy(idx[1][:, 0:1], small[:, 2:3]).then_inc(s_dve, 1)
                    dve.wait_ge(s_dve, e * per + (base + 6))
                    dve.wait_ge(s_tot, e + (n * ET + 1))
                    dve.tensor_tensor(slot_rows[1][:, 0, :], bank[5][:, 0:D], slot_rows[0][:, 1, :], ALU.add).then_inc(s_new, 1)
                    dve.wait_ge(s_scat[n], (e + 1) * 16)
                    passed(dve, "dve")
                count[0] += per * ET

            def phase(ph, general):
                l = LAYERS.index(ph) % 3 if ph != NORM else 0

                def slots_by_nodes(k, b, j):
                    return dve.tensor_scalar(onehot[k][:, GSTART[j]:GSTART[j + 1]], iota[:, 0:GW[j]],
                                             slot_place[:, bass.ds(b * GROUPS + j, 1)], None, ALU.is_equal)

                def first_onehot(t, k, b, last):
                    dve.wait_ge(s["summed"][k], before("summed", ph, t))
                    slots_by_nodes(k, b, 0)

                def other_onehots(t, k, b, last):
                    slots_by_nodes(k, b, 1)
                    slots_by_nodes(k, b, 2).then_inc(s["onehot"][k], 1)

                def sums_out(t, k, b, last):
                    dve.wait_ge(s["summed"][k], done("summed", ph, t))
                    dve.wait_ge(s["dense"][k], before("dense", ph, t))
                    if general:
                        dve.tensor_copy(sum_t[k][:, :], slot_sum[k % 2][:, :]).then_inc(s["sum_out"][k], 1)
                        return
                    dve.wait_ge(s["xt_out"][k], done("xt_out", ph, t))
                    dve.tensor_tensor(sum_t[k][:, :].rearrange("d (i p) -> d i p", i=RPP),
                                      slot_sum[k % 2][:, :].rearrange("d (p i) -> d i p", i=RPP),
                                      xt_sb[k][:, :].rearrange("d (i p) -> d i p", i=RPP), ALU.add).then_inc(s["sum_out"][k], 1)

                def prod_out(t, k, b, last):
                    dve.wait_ge(s["dense"][k], done("dense", ph, t))
                    dve.wait_ge(s["out_ready"][k], before("out_ready", ph, t))
                    for i in range(RPP):
                        at = slice(i * D, (i + 1) * D)
                        last_op = dve.scalar_tensor_tensor(part[k][:, at], prod[k % 2][:, at],
                                                           inv_deg[:, bass.ds(b * RPP + i, 1)], b_s[l][:, :], ALU.mult, ALU.add)
                    last_op.then_inc(s["prod_out"][k], 1)

                def combine(t, k, b, last):
                    dve.wait_ge(s["dense"][k], done("dense", ph, t))
                    if ph in (GCN1, GCN2):
                        dve.wait_ge(s["out_ready"][k], before("out_ready", ph, t))
                    if ph == GCN3:
                        dve.wait_ge(s["res_loaded"][k], done("res_loaded", ph, t))
                    if ph in SAGES:
                        dve.wait_ge(s["prod_out"][k], done("prod_out", ph, t))
                        dve.tensor_tensor(part[k][:, :], part[k][:, :], prod_x[k % 2][:, :], ALU.add)\
                           .then_inc(s["combined"][k], 1)
                        return
                    for i in range(RPP):
                        at = slice(i * D, (i + 1) * D)
                        other = res_rows[k][:, at] if ph == GCN3 else b_g[l][:, :]
                        last_op = dve.scalar_tensor_tensor(part[k][:, at], prod[k % 2][:, at],
                                                           norm_dst[:, bass.ds(b * RPP + i, 1)], other, ALU.mult, ALU.add)
                    last_op.then_inc(s["combined"][k], 1)

                def add_residual(t, k, b, last):
                    dve.wait_ge(s["combined"][k], done("combined", ph, t))
                    dve.wait_ge(s["res_loaded"][k], done("res_loaded", ph, t))
                    dve.tensor_tensor(res_rows[k][:, :], res_rows[k][:, :], part[k][:, :], ALU.add).then_inc(s["res_added"][k], 1)

                def add_bias(t, k, b, last):
                    dve.wait_ge(s["combined"][k], done("combined", ph, t))
                    dve.wait_ge(s["stored"][k], before("stored", ph, t))
                    dve.tensor_tensor(result[k][:, :].rearrange("p (i d) -> p i d", i=RPP),
                                      part[k][:, :].rearrange("p (i d) -> p i d", i=RPP),
                                      b_g[l][:, :].unsqueeze(1).to_broadcast([P, RPP, D]), ALU.add).then_inc(s["out_ready"][k], 1)

                def statistics(t, k, b, last):
                    if ph == NORM:
                        dve.wait_ge(s["x_loaded"][k], done("x_loaded", ph, t))
                        rows_in = x_rows
                    else:
                        dve.wait_ge(s["res_added"][k], done("res_added", ph, t))
                        rows_in = res_rows
                    dve.wait_ge(s["std"][k], before("std", ph, t))
                    for i in range(RPP):
                        last_op = dve.bn_stats(bn6[k][:, i, :], rows_in[k][:, i * D:(i + 1) * D])
                    last_op.then_inc(s["moments"][k], 1)

                def aggregate(t, k, b, last):
                    dve.wait_ge(s["moments"][k], done("moments", ph, t))
                    passed(dve, "dve")
                    for i in range(RPP):
                        last_op = dve.bn_aggr(mv[k][:, i, :], bn6[k][:, i, :])
                    last_op.then_inc(s["stats"][k], 1)

                def invert(t, k, b, last):
                    dve.wait_ge(s["std"][k], done("std", ph, t))
                    dve.wait_ge(s["out_ready"][k], before("out_ready", ph, t))
                    dve.reciprocal(scale[k][:, :], std[k][:, :]).then_inc(s["inverse"][k], 1)

                def scale_out(t, k, b, last):
                    dve.wait_ge(s["inverse"][k], done("inverse", ph, t))
                    dve.tensor_tensor(scale[k][:, :], scale[k][:, :], norm_src[:, bass.ds(b * RPP, RPP)], ALU.mult)\
                       .then_inc(s["scaled"][k], 1)

                def find_shift(t, k, b, last):
                    scaled = "scaled" if ph == SAGE3 else "inverse"
                    dve.wait_ge(s[scaled][k], done(scaled, ph, t))
                    dve.scalar_tensor_tensor(shift[k][:, :], mv[k][:, :, 0], -1.0, scale[k][:, :], ALU.mult, ALU.mult)\
                       .then_inc(s["rstd"][k], 1)

                if ph == NORM and general:
                    stages = [(0, invert), (1, statistics), (0, find_shift), (1, aggregate)]
                elif ph == NORM:
                    stages = [(0, invert), (1, statistics), (0, find_shift), (1, count_tile(0)), (1, aggregate),
                              (1, count_tile(1)), (1, count_tile(2))]
                elif ph == SAGE3:
                    stages = [(2, sums_out), (0, aggregate), (1, combine), (4, first_onehot), (0, invert), (1, add_residual),
                              (0, scale_out), (4, other_onehots), (0, find_shift), (1, statistics)]
                elif ph in SAGES:
                    stages = [(1, sums_out), (0, prod_out), (3, first_onehot), (3, other_onehots), (0, combine)]
                else:
                    stages = [(2, first_onehot), (2, other_onehots), (1, sums_out), (0, combine)]
                    if ph == GCN3:
                        stages.append((0, add_bias))
                for_blocks(dve, [x for x in stages if not (general and x[1] in (first_onehot, other_onehots))], ph)

            begin()
            check_edges()
            make_keys()
            cut_bias()
            steps_before = count[0]

            def fast():
                pick_slots()
                place_slots()
                phase(NORM, False)
                finish_counts()
                invert_degrees()
                for ph in LAYERS:
                    phase(ph, False)
                    if ph == SAGE1:
                        norms()

            def general():
                count[0] = steps_before
                phase(NORM, True)
                count_edges()
                invert_degrees()
                for ph in LAYERS:
                    add_messages(ph)
                    phase(ph, True)
                    if ph == SAGE1:
                        norms()

            if_slots(dve, fast, general)

        @block.tensor
        def _(pe):
            credit(pe, ["summed", "dense"])
            for k in range(4):
                pe.sem_inc(s_oh_used[k], GROUPS)
            pe.wait_ge(s_ready, 1)
            pe.matmul(bank[0][:, 0:ROWS], ones[0:1, :], first_f[:, :], start=True, stop=True).then_inc(s_firstb, 1)
            pe.wait_ge(s_chk, 1)
            pe.matmul(bank[1][0:1, 0:3], ones[:, 0:1], check3[:, 0:3], start=True, stop=True).then_inc(s_chksum, 1)

            def open_counts(banks, stop=False):
                for c in banks:
                    last_op = pe.matmul(bank[c][:, 0:HALF], zero16[0:1, 0:P], zero16[0:1, 0:HALF], start=not stop, stop=stop,
                                        skip_group_check=True)
                return last_op

            def count_slots():
                pe.wait_ge(s_keys, 1)
                for g in range(GB):
                    last_op = pe.transpose(bank[2 + g // 4][:, (g % 4) * P:(g % 4 + 1) * P], top[:, g, :], ident)
                last_op.then_inc(s_keys_t, 1)
                open_counts((6, 7))
                with pe.Fori(0, TURNS) as t:
                    for k in range(UN):
                        pe.wait_ge(s_degree_out, t * UN + (k + 1))
                        pe.wait_ge(s_pq[k], t + 1)
                        for j in range(GROUPS):
                            u = GROUPS * k + j
                            o = u % 4
                            pe.wait_ge(s_oh[o], t * GROUPS + (u // 4 + 1))
                            q = pe.matmul(bank[2 + k][:, 0:RPP], oh_pq[k][:, 0, j, :],
                                          oh_r[:, bass.ds(t * (UN * GROUPS) + u, 1), :].rearrange("p t r -> p (t r)"),
                                          start=j == 0, stop=j == GROUPS - 1, skip_group_check=True)
                            if j == GROUPS - 1:
                                q.then_inc(s_degree, 1)
                            for c in range(2):
                                last_op = pe.matmul(bank[6 + c][:, 0:HALF], oh_pq[k][:, 1, j, :], oh_c[o][:, c * HALF:(c + 1) * HALF],
                                                    start=False, stop=False, skip_group_check=True)
                            last_op.then_inc(s_oh_used[o], 1)
                open_counts((6, 7), True).then_inc(s_hist, 1)

            def count_edges():
                open_counts((4, 5, 6, 7))
                with pe.Fori(0, ET // GT) as h:
                    for k in range(GT):
                        pe.wait_ge(s_oh[k], h + 1)
                        for c in range(2):
                            at = slice(c * HALF, (c + 1) * HALF)
                            pe.matmul(bank[6 + c][:, 0:HALF], oh_p[k][:, :], oh_c[k][:, at], start=False, stop=False, skip_group_check=True)
                            o = pe.matmul(bank[4 + c][:, 0:HALF], oh_q[k][:, :], oh_d[k][:, at], start=False, stop=False, skip_group_check=True)
                        o.then_inc(s_oh_used[k], 1)
                open_counts((4, 5, 6, 7), True).then_inc(s_hist, 1)

            def add_messages(ph):
                n = LAYERS.index(ph)
                with pe.Fori(0, ET) as e:
                    pe.wait_ge(s_stage, e + (n * ET + 1))
                    pe.matmul(bank[4][:, 0:P], sum_t[0][:, 0:P], ident, start=True, stop=True).then_inc(s_spread, 1)
                    pe.wait_ge(s_eq, e + (n * ET + 1))
                    pe.wait_ge(s_gath[n], (e + 1) * 32)
                    pe.matmul(bank[5][:, 0:D], sum_t[1][:, 0:P], slot_rows[0][:, 0, :], start=True, stop=True).then_inc(s_tot, 1)

            def phase(ph, general):
                l = LAYERS.index(ph) % 3

                def front(t, k, b, last):
                    x_k, s_k = x_t[k % 2], slot_sum[k % 2]
                    pe.wait_ge(s["x_loaded"][k], done("x_loaded", ph, t))
                    wait_bank_free(pe, "sum_out", ph, t, k)
                    wait_bank_free(pe, "xt_out", ph, t, k)
                    for i in range(RPP):
                        at = slice(i * P, (i + 1) * P)
                        pe.transpose(x_k[:, at], x_rows[k][:, at], ident)
                    if general:
                        pe.wait_ge(s["agg_loaded"][k], done("agg_loaded", ph, t))
                        for i in range(RPP):
                            at = slice(i * P, (i + 1) * P)
                            last_op = pe.transpose(s_k[:, at], onehot[k][:, at], ident)
                    else:
                        pe.wait_ge(s["onehot"][k], done("onehot", ph, t))
                        pe.wait_ge(s["gathered"][k], done("gathered", ph, t))
                        for j in range(GROUPS):
                            at = slice(GSTART[j], GSTART[j + 1])
                            last_op = pe.matmul(s_k[:, at], slot_rows[k][:, j, :], onehot[k][:, at], start=True, stop=True)
                    last_op.then_inc(s["summed"][k], 1)

                def dense(t, k, b, last):
                    pe.wait_ge(s["sum_out"][k], done("sum_out", ph, t))
                    wait_bank_free(pe, "combined", ph, t, k)
                    w = w_l[l] if ph in SAGES else w_g[l]
                    for i in range(RPP):
                        at = slice(i * P, (i + 1) * P)
                        last_op = pe.matmul(prod[k % 2][:, at], sum_t[k][:, at], w[:, :], start=True, stop=True)
                    if ph in SAGES:
                        pe.wait_ge(s["xt_out"][k], done("xt_out", ph, t))
                        if ph == SAGE3:
                            pe.matmul(prod_x[k % 2][:, :], ones16[:, :], b_parts[:, :], start=True, stop=False,
                                      skip_group_check=True)
                        for i in range(RPP):
                            at = slice(i * P, (i + 1) * P)
                            last_op = pe.matmul(prod_x[k % 2][:, at], xt_sb[k][:, at], w_r[l][:, :], start=ph != SAGE3,
                                                stop=True, skip_group_check=True)
                    last_op.then_inc(s["dense"][k], 1)

                for_blocks(pe, [(1, front), (0, dense)], ph)

            def fast():
                count_slots()
                pe.wait_ge(s_tables, 1)
                for ph in LAYERS:
                    phase(ph, False)

            def general():
                count_edges()
                pe.wait_ge(s_tables, 1)
                for ph in LAYERS:
                    add_messages(ph)
                    phase(ph, True)

            if_slots(pe, fast, general)


_WEIGHTS = ["L0_gnn_Wl1", "L0_gnn_Wr1", "L0_gnn_Wl2", "L0_gnn_Wr2", "L0_gnn_Wl3", "L0_gnn_Wr3",
            "L1_gnn_W1", "L1_gnn_W2", "L1_gnn_W3"]
_BIASES = ["L0_gnn_bl1", "L0_gnn_bl2", "L0_gnn_bl3", "L1_gnn_b1", "L1_gnn_b2", "L1_gnn_b3"]


def make_program(nc):
    def given(name, shape, dt=F32):
        return nc.dram_tensor(name, shape, dt, kind="ExternalInput").ap()

    x, src, dst = given("x", [N, D]), given("src", [E], I32), given("dst", [E], I32)
    consts = given("consts", [P, C_ALL])
    w = [given(name, [D, D]) for name in _WEIGHTS]
    b = [given(name, [D]) for name in _BIASES]
    out = nc.dram_tensor("out", [N, D], F32, kind="ExternalOutput").ap()
    build(nc, x, src, dst, consts, w[0:6], b[0:3], w[6:9], b[3:6], out)


def kernel(**inputs):
    import concourse.bacc as bacc
    from concourse.bass_utils import run_bass_kernel_spmd

    nc = bacc.Bacc("TRN2", target_bir_lowering=False, num_devices=1)
    make_program(nc)
    arrays = {name: np.ascontiguousarray(inputs[name]) for name in ["x", "src", "dst"] + _WEIGHTS + _BIASES}
    arrays["consts"] = shape_constants()
    r = run_bass_kernel_spmd(nc, [arrays], core_ids=[0])
    return r.results[0]["out"]
```
